# Optimizing a Trainium2 kernel written in Bass

```python
import numpy as np
import jax
import jax.numpy as jnp

def _softmax(x, axis=-1):
    return jax.nn.softmax(x, axis=axis)

def _gelu(x):
    return jax.nn.gelu(x, approximate=True)

def _silu(x):
    return jax.nn.silu(x)

def _sigmoid(x):
    return jax.nn.sigmoid(x)

def _layernorm(x, axis=-1, eps=1e-05):
    m = jnp.mean(x, axis=axis, keepdims=True)
    v = jnp.var(x, axis=axis, keepdims=True)
    return (x - m) / jnp.sqrt(v + eps)

def _scatter_add(tgt, idx, src, axis=0):
    return tgt.at[idx].add(src)

def _segment_sum(src, seg, n):
    return jax.ops.segment_sum(src, seg, n)
kernel_name = 'mk_cond_seq_d4_seqx_r8_f8cfad'

def setup_inputs(seed: int=0):
    np.random.seed(seed)
    _w = jnp.asarray

    def _rec_inputs():
        import jax
        import jax.numpy as jnp
        _rk = jax.random.key(seed)
        x = 1.648e-05 + 1 * jax.random.normal(jax.random.fold_in(_rk, 1), (32, 128, 144), jnp.float32)
        _lenS = 128 - jax.random.randint(jax.random.fold_in(_rk, 7), (32,), 0, max(1, 128 // 4) + 1, jnp.int32)
        _lenS2 = 128 - jax.random.randint(jax.random.fold_in(_rk, 8), (32,), 0, max(1, 128 // 4) + 1, jnp.int32)
        cond_1152 = 0.00914911 + 1.00357 * jax.random.normal(jax.random.fold_in(_rk, 11), (32, 144), jnp.float32)
        return (x, cond_1152)
    x, cond_1152 = _rec_inputs()

    def _L0_cond_setup():
        import jax, jax.numpy as jnp
        import numpy as np
        B, L, C = (8, 128, 144)
        H = 16
        D = C // H
        FF = int(C * 4.0)
        EPS = 1e-06

        def _layernorm(x):
            mu = jnp.mean(x, axis=-1, keepdims=True)
            var = jnp.mean(jnp.square(x - mu), axis=-1, keepdims=True)
            return (x - mu) * jax.lax.rsqrt(var + EPS)

        def _modulate(x, shift, scale):
            return x * (1.0 + scale) + shift

        def _attention(h, W_qkv, b_qkv, W_proj, b_proj):
            b, l, c = h.shape
            qkv = h @ W_qkv + b_qkv
            qkv = qkv.reshape(b, l, 3, H, D)
            q, k, v = (qkv[:, :, 0], qkv[:, :, 1], qkv[:, :, 2])
            scale = D ** (-0.5)
            scores = jnp.einsum('blhd,bmhd->bhlm', q * scale, k)
            attn = jax.nn.softmax(scores, axis=-1)
            o = jnp.einsum('bhlm,bmhd->blhd', attn, v).reshape(b, l, c)
            return o @ W_proj + b_proj
        key = jax.random.key(seed)
        ks = jax.random.split(key, 12)
        s = 0.02
        return {'x': jax.random.normal(ks[0], (B, L, C), jnp.float32), 'c': jax.random.normal(ks[1], (B, 1, C), jnp.float32), 'W_qkv': jax.random.normal(ks[2], (C, 3 * C), jnp.float32) * s, 'b_qkv': jnp.zeros((3 * C,), jnp.float32), 'W_proj': jax.random.normal(ks[3], (C, C), jnp.float32) * s, 'b_proj': jnp.zeros((C,), jnp.float32), 'W_fc1': jax.random.normal(ks[4], (C, FF), jnp.float32) * s, 'b_fc1': jnp.zeros((FF,), jnp.float32), 'W_fc2': jax.random.normal(ks[5], (FF, C), jnp.float32) * s, 'b_fc2': jnp.zeros((C,), jnp.float32), 'W_ada': jax.random.normal(ks[6], (C, 6 * C), jnp.float32) * s, 'b_ada': jnp.zeros((6 * C,), jnp.float32)}
    _L0_cond_all = _L0_cond_setup()
    _L0_cond_in = {k: v for k, v in _L0_cond_all.items() if k in ('W_qkv', 'b_qkv', 'W_proj', 'b_proj', 'W_fc1', 'b_fc1', 'W_fc2', 'b_fc2', 'W_ada', 'b_ada')}
    del _L0_cond_all

    def _L1_cond_setup():
        import jax, jax.numpy as jnp
        import numpy as np
        NUM_HEADS = 16
        NUM_EXPERTS = 4
        TOP_K = 2
        LN_EPS = 1e-06

        def _ln(h):
            mu = jnp.mean(h, axis=-1, keepdims=True)
            var = jnp.var(h, axis=-1, keepdims=True)
            return (h - mu) * jax.lax.rsqrt(var + LN_EPS)

        def _modulate(h, shift, scale):
            return h * (1.0 + scale[:, None, :]) + shift[:, None, :]
        key = jax.random.key(seed)
        ks = jax.random.split(key, 12)
        B, N, C = (8, 128, 144)
        H = 4 * C
        E = NUM_EXPERTS
        s = 0.02
        return {'x': jax.random.normal(ks[0], (B, N, C), jnp.float32), 'c': jax.random.normal(ks[1], (B, C), jnp.float32), 'w_adaln': jax.random.normal(ks[2], (C, 6 * C), jnp.float32) * s, 'b_adaln': jnp.zeros((6 * C,), jnp.float32), 'w_qkv': jax.random.normal(ks[3], (C, 3 * C), jnp.float32) * s, 'b_qkv': jnp.zeros((3 * C,), jnp.float32), 'w_proj': jax.random.normal(ks[4], (C, C), jnp.float32) * s, 'b_proj': jnp.zeros((C,), jnp.float32), 'w_gate': jax.random.normal(ks[5], (C, E), jnp.float32) * s, 'w1': jax.random.normal(ks[6], (E, C, H), jnp.float32) * s, 'b1': jnp.zeros((E, H), jnp.float32), 'w2': jax.random.normal(ks[7], (E, H, C), jnp.float32) * s, 'b2': jnp.zeros((E, C), jnp.float32)}
    _L1_cond_all = _L1_cond_setup()
    _L1_cond_in = {k: v for k, v in _L1_cond_all.items() if k in ('w_adaln', 'b_adaln', 'w_qkv', 'b_qkv', 'w_proj', 'b_proj', 'w_gate', 'w1', 'b1', 'w2', 'b2')}
    del _L1_cond_all

    def _L2_cond_setup():
        import jax, jax.numpy as jnp
        import numpy as np
        B, S, D = (8, 128, 144)
        H = 16
        HD = D // H
        HID = int(D * 4.0)
        LN_EPS = 1e-05

        def layer_norm(x, w, b):
            m = jnp.mean(x, axis=-1, keepdims=True)
            v = jnp.mean(jnp.square(x - m), axis=-1, keepdims=True)
            return (x - m) * jax.lax.rsqrt(v + LN_EPS) * w + b

        def modulate(x, shift, scale):
            return x * (1.0 + scale[:, None, :]) + shift[:, None, :]

        def attention(x, wq, wk, wv, wo, wo_b):
            b, s, d = x.shape
            q = (x @ wq).reshape(b, s, H, HD).transpose(0, 2, 1, 3)
            k = (x @ wk).reshape(b, s, H, HD).transpose(0, 2, 1, 3)
            v = (x @ wv).reshape(b, s, H, HD).transpose(0, 2, 1, 3)
            scale = 1.0 / np.sqrt(HD).astype(np.float32)
            att = jnp.einsum('bhqd,bhkd->bhqk', q, k) * scale
            att = jax.nn.softmax(att, axis=-1)
            out = jnp.einsum('bhqk,bhkd->bhqd', att, v)
            out = out.transpose(0, 2, 1, 3).reshape(b, s, d)
            return out @ wo + wo_b
        key = jax.random.key(seed)
        ks = jax.random.split(key, 16)
        s = 0.02
        return {'x': jax.random.normal(ks[0], (B, S, D), jnp.float32), 'c': jax.random.normal(ks[1], (B, D), jnp.float32), 'ln1_w': jnp.ones((D,), jnp.float32), 'ln1_b': jnp.zeros((D,), jnp.float32), 'wq': jax.random.normal(ks[2], (D, D), jnp.float32) * s, 'wk': jax.random.normal(ks[3], (D, D), jnp.float32) * s, 'wv': jax.random.normal(ks[4], (D, D), jnp.float32) * s, 'wo': jax.random.normal(ks[5], (D, D), jnp.float32) * s, 'wo_b': jnp.zeros((D,), jnp.float32), 'ln2_w': jnp.ones((D,), jnp.float32), 'ln2_b': jnp.zeros((D,), jnp.float32), 'fc1_w': jax.random.normal(ks[6], (D, HID), jnp.float32) * s, 'fc1_b': jnp.zeros((HID,), jnp.float32), 'fc2_w': jax.random.normal(ks[7], (HID, D), jnp.float32) * s, 'fc2_b': jnp.zeros((D,), jnp.float32), 'ada_w': jax.random.normal(ks[8], (D, 6 * D), jnp.float32) * s, 'ada_b': jnp.zeros((6 * D,), jnp.float32)}
    _L2_cond_all = _L2_cond_setup()
    _L2_cond_in = {k: v for k, v in _L2_cond_all.items() if k in ('ln1_w', 'ln1_b', 'wq', 'wk', 'wv', 'wo', 'wo_b', 'ln2_w', 'ln2_b', 'fc1_w', 'fc1_b', 'fc2_w', 'fc2_b', 'ada_w', 'ada_b')}
    del _L2_cond_all

    def _L3_cond_setup():
        import jax, jax.numpy as jnp
        import numpy as np
        from jax.scipy.linalg import expm
        N, D, COND_DIM = (144, 64, 144)
        B, T = (16, 128)

        def _rotation(cond, W, b):
            v = jax.nn.silu(cond) @ W.T + b
            iu, ju = jnp.triu_indices(D, k=1)
            A = jnp.zeros((cond.shape[0], D, D), dtype=v.dtype)
            A = A.at[:, iu, ju].set(v).at[:, ju, iu].set(-v)
            return expm(A)
        key = jax.random.key(seed)
        k1, k2, k3, k4, k5 = jax.random.split(key, 5)
        x = jax.random.normal(k1, (B, T, N), dtype=jnp.float32)
        cond = jax.random.normal(k2, (B, COND_DIM), dtype=jnp.float32)
        P = jax.random.normal(k3, (N, D), dtype=jnp.float32)
        n_skew = D * (D - 1) // 2
        bound = 1.0 / np.sqrt(COND_DIM)
        W = jax.random.uniform(k4, (n_skew, COND_DIM), minval=-bound, maxval=bound, dtype=jnp.float32)
        b = jax.random.uniform(k5, (n_skew,), minval=-bound, maxval=bound, dtype=jnp.float32)
        return {'x': x, 'cond': cond, 'P': P, 'W': W, 'b': b}
    _L3_cond_all = _L3_cond_setup()
    _L3_cond_in = {k: v for k, v in _L3_cond_all.items() if k in ('P', 'W', 'b')}
    del _L3_cond_all
    return {'x': x, 'cond_1152': cond_1152, 'L0_cond_W_qkv': _L0_cond_in['W_qkv'], 'L0_cond_b_qkv': _L0_cond_in['b_qkv'], 'L0_cond_W_proj': _L0_cond_in['W_proj'], 'L0_cond_b_proj': _L0_cond_in['b_proj'], 'L0_cond_W_fc1': _L0_cond_in['W_fc1'], 'L0_cond_b_fc1': _L0_cond_in['b_fc1'], 'L0_cond_W_fc2': _L0_cond_in['W_fc2'], 'L0_cond_b_fc2': _L0_cond_in['b_fc2'], 'L0_cond_W_ada': _L0_cond_in['W_ada'], 'L0_cond_b_ada': _L0_cond_in['b_ada'], 'L1_cond_w_adaln': _L1_cond_in['w_adaln'], 'L1_cond_b_adaln': _L1_cond_in['b_adaln'], 'L1_cond_w_qkv': _L1_cond_in['w_qkv'], 'L1_cond_b_qkv': _L1_cond_in['b_qkv'], 'L1_cond_w_proj': _L1_cond_in['w_proj'], 'L1_cond_b_proj': _L1_cond_in['b_proj'], 'L1_cond_w_gate': _L1_cond_in['w_gate'], 'L1_cond_w1': _L1_cond_in['w1'], 'L1_cond_b1': _L1_cond_in['b1'], 'L1_cond_w2': _L1_cond_in['w2'], 'L1_cond_b2': _L1_cond_in['b2'], 'L2_cond_ln1_w': _L2_cond_in['ln1_w'], 'L2_cond_ln1_b': _L2_cond_in['ln1_b'], 'L2_cond_wq': _L2_cond_in['wq'], 'L2_cond_wk': _L2_cond_in['wk'], 'L2_cond_wv': _L2_cond_in['wv'], 'L2_cond_wo': _L2_cond_in['wo'], 'L2_cond_wo_b': _L2_cond_in['wo_b'], 'L2_cond_ln2_w': _L2_cond_in['ln2_w'], 'L2_cond_ln2_b': _L2_cond_in['ln2_b'], 'L2_cond_fc1_w': _L2_cond_in['fc1_w'], 'L2_cond_fc1_b': _L2_cond_in['fc1_b'], 'L2_cond_fc2_w': _L2_cond_in['fc2_w'], 'L2_cond_fc2_b': _L2_cond_in['fc2_b'], 'L2_cond_ada_w': _L2_cond_in['ada_w'], 'L2_cond_ada_b': _L2_cond_in['ada_b'], 'L3_cond_P': _L3_cond_in['P'], 'L3_cond_W': _L3_cond_in['W'], 'L3_cond_b': _L3_cond_in['b']}

def reference(x, cond_1152, L0_cond_W_qkv, L0_cond_b_qkv, L0_cond_W_proj, L0_cond_b_proj, L0_cond_W_fc1, L0_cond_b_fc1, L0_cond_W_fc2, L0_cond_b_fc2, L0_cond_W_ada, L0_cond_b_ada, L1_cond_w_adaln, L1_cond_b_adaln, L1_cond_w_qkv, L1_cond_b_qkv, L1_cond_w_proj, L1_cond_b_proj, L1_cond_w_gate, L1_cond_w1, L1_cond_b1, L1_cond_w2, L1_cond_b2, L2_cond_ln1_w, L2_cond_ln1_b, L2_cond_wq, L2_cond_wk, L2_cond_wv, L2_cond_wo, L2_cond_wo_b, L2_cond_ln2_w, L2_cond_ln2_b, L2_cond_fc1_w, L2_cond_fc1_b, L2_cond_fc2_w, L2_cond_fc2_b, L2_cond_ada_w, L2_cond_ada_b, L3_cond_P, L3_cond_W, L3_cond_b):
    import jax
    import jax.numpy as jnp

    def _L0_cond_ref(x, c, W_qkv, b_qkv, W_proj, b_proj, W_fc1, b_fc1, W_fc2, b_fc2, W_ada, b_ada):
        import jax, jax.numpy as jnp
        import numpy as np
        B, L, C = (8, 128, 144)
        H = 16
        D = C // H
        FF = int(C * 4.0)
        EPS = 1e-06

        def _layernorm(x):
            mu = jnp.mean(x, axis=-1, keepdims=True)
            var = jnp.mean(jnp.square(x - mu), axis=-1, keepdims=True)
            return (x - mu) * jax.lax.rsqrt(var + EPS)

        def _modulate(x, shift, scale):
            return x * (1.0 + scale) + shift

        def _attention(h, W_qkv, b_qkv, W_proj, b_proj):
            b, l, c = h.shape
            qkv = h @ W_qkv + b_qkv
            qkv = qkv.reshape(b, l, 3, H, D)
            q, k, v = (qkv[:, :, 0], qkv[:, :, 1], qkv[:, :, 2])
            scale = D ** (-0.5)
            scores = jnp.einsum('blhd,bmhd->bhlm', q * scale, k)
            attn = jax.nn.softmax(scores, axis=-1)
            o = jnp.einsum('bhlm,bmhd->blhd', attn, v).reshape(b, l, c)
            return o @ W_proj + b_proj
        ada = jax.nn.silu(c) @ W_ada + b_ada
        shift_msa, scale_msa, gate_msa, shift_mlp, scale_mlp, gate_mlp = jnp.split(ada, 6, axis=-1)
        h = _modulate(_layernorm(x), shift_msa, scale_msa)
        x = x + gate_msa * _attention(h, W_qkv, b_qkv, W_proj, b_proj)
        h = _modulate(_layernorm(x), shift_mlp, scale_mlp)
        mlp = jax.nn.gelu(h @ W_fc1 + b_fc1, approximate=True) @ W_fc2 + b_fc2
        x = x + gate_mlp * mlp
        return x

    def _L1_cond_ref(x, c, w_adaln, b_adaln, w_qkv, b_qkv, w_proj, b_proj, w_gate, w1, b1, w2, b2):
        import jax, jax.numpy as jnp
        import numpy as np
        NUM_HEADS = 16
        NUM_EXPERTS = 4
        TOP_K = 2
        LN_EPS = 1e-06

        def _ln(h):
            mu = jnp.mean(h, axis=-1, keepdims=True)
            var = jnp.var(h, axis=-1, keepdims=True)
            return (h - mu) * jax.lax.rsqrt(var + LN_EPS)

        def _modulate(h, shift, scale):
            return h * (1.0 + scale[:, None, :]) + shift[:, None, :]
        B, N, C = x.shape
        nh = NUM_HEADS
        hd = C // nh
        mod = jax.nn.silu(c) @ w_adaln + b_adaln
        sh_msa, sc_msa, g_msa, sh_mlp, sc_mlp, g_mlp = jnp.split(mod, 6, axis=-1)
        h = _modulate(_ln(x), sh_msa, sc_msa)
        qkv = (h @ w_qkv + b_qkv).reshape(B, N, 3, nh, hd).transpose(2, 0, 3, 1, 4)
        q, k, v = (qkv[0], qkv[1], qkv[2])
        attn = jax.nn.softmax(jnp.einsum('bhqd,bhkd->bhqk', q, k) * hd ** (-0.5), axis=-1)
        o = jnp.einsum('bhqk,bhkd->bhqd', attn, v).transpose(0, 2, 1, 3).reshape(B, N, C)
        o = o @ w_proj + b_proj
        x = x + g_msa[:, None, :] * o
        xn = _modulate(_ln(x), sh_mlp, sc_mlp)
        xf = xn.reshape(-1, C)
        gate_logits = xf @ w_gate
        topk_logits, topk_idx = jax.lax.top_k(gate_logits, TOP_K)
        gates = jax.nn.softmax(topk_logits, axis=-1)
        cw = jnp.sum(jax.nn.one_hot(topk_idx, NUM_EXPERTS, dtype=xf.dtype) * gates[..., None], axis=1)
        hmid = jax.nn.gelu(jnp.einsum('tc,ech->eth', xf, w1) + b1[:, None, :], approximate=True)
        eo = jnp.einsum('eth,ehc->etc', hmid, w2) + b2[:, None, :]
        moe = jnp.einsum('te,etc->tc', cw, eo).reshape(B, N, C)
        return x + g_mlp[:, None, :] * moe

    def _L2_cond_ref(x, c, ln1_w, ln1_b, wq, wk, wv, wo, wo_b, ln2_w, ln2_b, fc1_w, fc1_b, fc2_w, fc2_b, ada_w, ada_b):
        import jax, jax.numpy as jnp
        import numpy as np
        B, S, D = (8, 128, 144)
        H = 16
        HD = D // H
        HID = int(D * 4.0)
        LN_EPS = 1e-05

        def layer_norm(x, w, b):
            m = jnp.mean(x, axis=-1, keepdims=True)
            v = jnp.mean(jnp.square(x - m), axis=-1, keepdims=True)
            return (x - m) * jax.lax.rsqrt(v + LN_EPS) * w + b

        def modulate(x, shift, scale):
            return x * (1.0 + scale[:, None, :]) + shift[:, None, :]

        def attention(x, wq, wk, wv, wo, wo_b):
            b, s, d = x.shape
            q = (x @ wq).reshape(b, s, H, HD).transpose(0, 2, 1, 3)
            k = (x @ wk).reshape(b, s, H, HD).transpose(0, 2, 1, 3)
            v = (x @ wv).reshape(b, s, H, HD).transpose(0, 2, 1, 3)
            scale = 1.0 / np.sqrt(HD).astype(np.float32)
            att = jnp.einsum('bhqd,bhkd->bhqk', q, k) * scale
            att = jax.nn.softmax(att, axis=-1)
            out = jnp.einsum('bhqk,bhkd->bhqd', att, v)
            out = out.transpose(0, 2, 1, 3).reshape(b, s, d)
            return out @ wo + wo_b
        mod = jax.nn.silu(c) @ ada_w + ada_b
        sh_msa, sc_msa, g_msa, sh_mlp, sc_mlp, g_mlp = jnp.split(mod, 6, axis=1)
        h = modulate(layer_norm(x, ln1_w, ln1_b), sh_msa, sc_msa)
        x = x + g_msa[:, None, :] * attention(h, wq, wk, wv, wo, wo_b)
        h = modulate(layer_norm(x, ln2_w, ln2_b), sh_mlp, sc_mlp)
        h = jax.nn.gelu(h @ fc1_w + fc1_b, approximate=False) @ fc2_w + fc2_b
        x = x + g_mlp[:, None, :] * h
        return x

    def _L3_cond_ref(x, cond, P, W, b):
        import jax, jax.numpy as jnp
        import numpy as np
        from jax.scipy.linalg import expm
        N, D, COND_DIM = (144, 64, 144)
        B, T = (16, 128)

        def _rotation(cond, W, b):
            v = jax.nn.silu(cond) @ W.T + b
            iu, ju = jnp.triu_indices(D, k=1)
            A = jnp.zeros((cond.shape[0], D, D), dtype=v.dtype)
            A = A.at[:, iu, ju].set(v).at[:, ju, iu].set(-v)
            return expm(A)
        U, _ = jnp.linalg.qr(P)
        R = _rotation(cond, W, b)
        z = jnp.einsum('btn,nd->btd', x, U)
        z_rot = jnp.einsum('btd,bde->bte', z, R)
        x_rot = x + jnp.einsum('btd,nd->btn', z_rot - z, U)
        return x_rot
    x = _L0_cond_ref(x, cond_1152[:, None, :], L0_cond_W_qkv, L0_cond_b_qkv, L0_cond_W_proj, L0_cond_b_proj, L0_cond_W_fc1, L0_cond_b_fc1, L0_cond_W_fc2, L0_cond_b_fc2, L0_cond_W_ada, L0_cond_b_ada)
    x = _L1_cond_ref(x, cond_1152, L1_cond_w_adaln, L1_cond_b_adaln, L1_cond_w_qkv, L1_cond_b_qkv, L1_cond_w_proj, L1_cond_b_proj, L1_cond_w_gate, L1_cond_w1, L1_cond_b1, L1_cond_w2, L1_cond_b2)
    x = _L2_cond_ref(x, cond_1152, L2_cond_ln1_w, L2_cond_ln1_b, L2_cond_wq, L2_cond_wk, L2_cond_wv, L2_cond_wo, L2_cond_wo_b, L2_cond_ln2_w, L2_cond_ln2_b, L2_cond_fc1_w, L2_cond_fc1_b, L2_cond_fc2_w, L2_cond_fc2_b, L2_cond_ada_w, L2_cond_ada_b)
    x = _L3_cond_ref(x, cond_1152, L3_cond_P, L3_cond_W, L3_cond_b)
    return x

_drawn_inputs = setup_inputs


def setup_inputs(seed=0):
    import zlib

    import numpy as np

    out = dict(_drawn_inputs(seed))
    spreads = {'L0_cond_b_qkv': (0.0, 0.8),
     'L0_cond_b_proj': (0.0, 0.472),
     'L0_cond_b_fc1': (0.0, 0.8),
     'L0_cond_b_fc2': (0.0, 0.479),
     'L0_cond_b_ada': (0.0, 0.499),
     'L1_cond_b_adaln': (0.0, 0.558),
     'L1_cond_b_qkv': (0.0, 0.8),
     'L1_cond_b_proj': (0.0, 0.442),
     'L1_cond_b1': (0.0, 0.8),
     'L1_cond_b2': (0.0, 0.676),
     'L2_cond_ln1_w': (1.0, 0.6),
     'L2_cond_ln1_b': (0.0, 0.8),
     'L2_cond_wo_b': (0.0, 0.409),
     'L2_cond_ln2_w': (1.0, 0.6),
     'L2_cond_ln2_b': (0.0, 0.8),
     'L2_cond_fc1_b': (0.0, 0.8),
     'L2_cond_fc2_b': (0.0, 0.501),
     'L2_cond_ada_b': (0.0, 0.514)}
    factors = {'L0_cond_W_qkv': 8.0,
     'L0_cond_W_proj': 8.0,
     'L0_cond_W_fc1': 5.324,
     'L0_cond_W_fc2': 4.959,
     'L1_cond_w_adaln': 2.918,
     'L1_cond_w_qkv': 8.0,
     'L1_cond_w_proj': 8.0,
     'L1_cond_w_gate': 5.807,
     'L1_cond_w1': 7.658,
     'L1_cond_w2': 7.133,
     'L2_cond_wq': 8.0,
     'L2_cond_wk': 8.0,
     'L2_cond_wv': 8.0,
     'L2_cond_wo': 8.0,
     'L2_cond_fc1_w': 4.937,
     'L2_cond_fc2_w': 4.455}
    for name, (base, spread) in spreads.items():
        noise = np.random.default_rng([zlib.crc32(name.encode()), seed]).standard_normal(out[name].shape)
        drawn = base * np.exp(spread * noise) if base else spread * noise
        out[name] = jnp.asarray(drawn.astype(out[name].dtype))
    for name, factor in factors.items():
        out[name] = (out[name] * factor).astype(out[name].dtype)
    return out
```

```python
import numpy as np
import concourse.bass as bass
from concourse import mybir
from contextlib import ExitStack

F32 = mybir.dt.float32
F32R = mybir.dt.float32r
ALU = mybir.AluOpType
ACT = mybir.ActivationFunctionType
AX = mybir.AxisListType

NB, T, C = 32, 128, 144
NH, HD = 16, 9
LAYERS = 3
C0 = 128
C1 = C - C0 + 1
S3 = 3 * C1
XW = C0 + S3
G, HG, HP = 4, 4, 32
WQKV = 2 * G * 128 + C
FF = 4 * C
NE = 4
EXPERTS = (1, NE, 1)
FTILES = ((5,), (5, 4, 5, 4), (5,))
FTOT = tuple(sum(f) for f in FTILES)
WM = (FF, NE * FF + NE, FF)
WMX = max(WM)
FT = 5
MT = 4
NM = NB // MT
RD = 64
SQUARINGS = 6
EPS = (1e-6, 1e-6, 1e-5)
GC = LAYERS * 2 * C
SPLIT_PIECES = (WMX + 511) // 512
SPLITS = 2 + 2 * SPLIT_PIECES
NHALF = NB // 2
K_ID, K_MQ, K_MK, K_MH, K_MW, K_IOTA, K_EYE, K_SGN, K_LOW = 0, 128, 129, 130, 131, 132, 133, 197, 261
K_N = K_LOW + NE * NE
FWD, BWD = 15, 6
RADD = bass.bass_isa.ReduceOp.add


def wait(eng, sem, value):
    if isinstance(value, int) and value <= 0:
        return
    eng.wait_ge(sem, value)


def cut(start, size):
    return slice(start, start + size) if isinstance(start, int) else bass.ds(start, size)


def program(nc, d, out, gates_dram, skew_dram):
    ctx = ExitStack()
    with ctx:
        def sb(name, shape, dt=F32):
            return ctx.enter_context(nc.sbuf_tensor(name, shape, dt))

        def sem(name):
            return ctx.enter_context(nc.semaphore(name))

        X = sb("X", [128, NB * C])
        K = sb("K", [128, K_N])
        ident = K[:, K_ID:K_ID + 128]
        st6 = sb("st6", [128, NB, 6])
        mean = sb("mean", [128, NB])
        var = sb("var", [128, NB])
        rstd = sb("rstd", [128, NB])
        rtmp = sb("rtmp", [128, 3, NB])
        epst = sb("epst", [128, 3])
        sc0, sc1 = sb("sc0", [C0, NB]), sb("sc1", [C1, NB])
        ctmp = sb("ctmp", [128, 4, NB])
        col0 = sb("col0", [C0, LAYERS, 4, NB])
        col1 = sb("col1", [S3, LAYERS, 4, NB])
        lnc = sb("lnc", [128, 8])
        Whi, Wlo = sb("Whi", [C0, WMX], F32R), sb("Wlo", [C0, WMX], F32R)
        W3 = sb("W3", [S3, WMX], F32R)
        wp0, wp1 = sb("wp0", [C0, 2, C]), sb("wp1", [C1, 2, C])
        w2 = sb("w2", [128, NE * FT, C])
        b2 = sb("b2", [1, NE, C])
        ones = sb("ones", [1, 128])
        xh = sb("xh", [128, 2 * MT, XW])
        hf = sb("hf", [128, MT * 128])
        hs = sb("hs", [S3, MT * 128])
        hshi = sb("hshi", [S3, MT * 128], F32R)
        hhi, hlo = sb("hhi", [128, 2, MT * 128], F32R), sb("hlo", [128, 2, MT * 128], F32R)
        h3 = sb("h3", [S3, 2, MT * 128], F32R)
        Q = sb("Q", [128, 2, G, 256], F32R)
        kst = sb("kst", [128, 512], F32R)
        KBD = sb("KBD", [128, 2, G, HG, 256], F32R)
        qkhi = sb("qkhi", [128, 512], F32R)
        nmax = sb("nmax", [128, 2, NH])
        mT = sb("mT", [NH, 2, 128], F32R)
        gate = sb("gate", [128, 4, C])
        ytmp = sb("ytmp", [128, C])
        BIG = sb("BIG", [128, 10240 + 2 * WMX])
        VA = BIG[:, 0:2048].rearrange("p (b h w) -> p b h w", b=4, h=NH)
        PT = BIG[:, 2048:6144].rearrange("p (b r n) -> p b r n", b=2, r=HG)
        OTs = BIG[:, 6144:7168].rearrange("p (b n) -> p b n", b=2)
        oq = BIG[:, 7168:7168 + 2 * (C + 1)].rearrange("p (b n) -> p b n", b=2)
        oT = BIG[:, 7500:8012].rearrange("p (b n) -> p b n", b=2)
        rsum = BIG[:, 8012:8044].rearrange("p (b n) -> p b n", b=2)
        hm = BIG[:, 0:9216].rearrange("p (t n) -> p t n", n=512)
        acc = BIG[:, 9216:9792]
        rt = BIG[:, 9792:10240]
        RAW0 = 10240
        WR = BIG[:, RAW0:RAW0 + WMX]
        WR3 = BIG[0:S3, RAW0 + WMX:RAW0 + 2 * WMX]
        gate_rows = BIG[0:NB, 9000:9000 + GC]
        mgate = sb("mgate", [128, 2, MT * C])

        QA, QV, QU = (sb(n, [128, 2, RD]) for n in ("QA", "QV", "QU"))
        qprod, qsum, qtmp, qw, qtau = (sb("qprod", [128, 2 * RD]), sb("qsum", [128, 2 * RD]), sb("qtmp", [128, 2, RD]),
                                       sb("qw", [128, RD]), sb("qtau", [128, RD]))
        qk_, qs, qc = sb("qcount", [128, 1]), sb("qscalars", [128, 8]), sb("qexponents", [128, 2])
        UD = BIG[:, 12288:12288 + 4 * RD].rearrange("p (k j) -> p k j", k=2)
        UT = BIG[:, 12544:12544 + C]
        SW0, SW1 = BIG[:, RAW0:RAW0 + RD * RD], BIG[0:C1, RD * RD:2 * RD * RD]
        SV = BIG[0:NB, 0:RD * RD]
        M = [BIG[:, RD * RD + k * NHALF * RD:RD * RD + (k + 1) * NHALF * RD].rearrange("p (n j) -> p n j", n=NHALF)
             for k in range(8)]
        FM = M[1:5]
        xT0, xT1 = BIG[:, 0:1024], BIG[0:C - C0, 1024:2048]
        zs, ys = BIG[:, 2048:3072], BIG[:, 3072:4096]

        PS = [ctx.enter_context(nc.psum_tensor(f"PS{n}", [128, 512], F32)) for n in range(8)]

        ld_cond, ld_ada, ld_gw, ld_x, ld_skew = (sem("cond_loaded"), sem("ada_loaded"), sem("gate_weights_loaded"),
                                                       sem("x_loaded"), sem("skew_loaded"))
        ld_wq, ld_wm, ld_wp, ld_w2 = sem("wqkv_loaded"), sem("wm_loaded"), sem("wp_loaded"), sem("w2_loaded")
        s_split = sem("weights_split")
        s_e, s_silu, s_ones, s_const = sem("cond_exp"), sem("silu_steps"), sem("ones_set"), sem("constants_set")
        s_gps, s_gev, s_gst, s_cps, s_cev = (sem("gates_product"), sem("gates_copied"), sem("gates_stored"),
                                             sem("columns_product"), sem("columns_ready"))
        s_cln = sem("columns_steps")
        s_st0, s_var, s_std, s_ln = sem("first_stats"), sem("variance_ready"), sem("std_ready"), sem("rstd_steps")
        xh_ready, xt_done = sem("xh_ready"), sem("xt_done")
        hf_ready, hhi_ready, h_ready = sem("hf_ready"), sem("hhi_ready"), sem("h_ready")
        qk_ps, qk_hi, qk_lo = sem("qk_product"), sem("qk_high"), sem("qk_stacked")
        v_ps, v_ev, va_set = sem("v_product"), sem("v_ready"), sem("va_set")
        s1_done, max_done = sem("s1_done"), sem("max_done")
        mt_done, mt_ev, mrow = sem("max_transposed"), sem("max_copied"), sem("max_row_written")
        s2_done, exp_done = sem("s2_done"), sem("exp_done")
        pv_done, ot_ev = sem("pv_done"), sem("ot_copied")
        otr_done, rs_done, norm_done = sem("o_back"), sem("rsum_done"), sem("o_normalised")
        ot2_done, oT_ev = sem("o_transposed"), sem("oT_copied")
        y_done, y_read, x_new, res_done = (sem("proj_done"), sem("y_gated"), sem("x_updated"),
                                            sem("res_done"))
        gate_ld = [sem(f"gate_loaded{n}") for n in range(4)]
        kbd_a, kbd_v = sem("kbd_by_act"), sem("kbd_by_dve")
        f1_done, gelu_done = sem("fc1_done"), sem("gelu_done")
        f2_done, acc_done = sem("fc2_done"), sem("expert_added")
        hm_ones = sem("hm_ones_set")
        g_ps, g_steps, g_th = sem("router_product"), sem("router_steps"), sem("router_tanh")
        m_gate = [sem("mlp_gate_loaded0"), sem("mlp_gate_loaded1")]

        q_ld, q_step, qr_done = sem("p_loaded"), sem("qr_step"), sem("u_ready")
        sk_ps, sk_ev0, sk_ev1, sk_st, sk_ld = (sem("skew_product"), sem("skew_copied_by_dve"), sem("skew_copied_by_act"),
                                       sem("skew_stored"), sem("skew_back"))
        r_ps, r_ev = sem("matrix_product"), sem("matrix_step")
        u_dup, u_ps, u_ev = sem("u_doubled"), sem("u_turned"), sem("ut_ready")
        t_ps, t_ev, z_ps, z_ev, yy_ps, yy_ev, o_ps, o_ev, s_out = (
            sem("x_turned"), sem("xT_copied"), sem("z_product"), sem("z_copied"), sem("zr_product"), sem("zr_copied"),
            sem("rotated"), sem("x_rotated"), sem("output_stored"))

        def n_batch(l, mlp):
            return (2 * l + mlp) * NB

        def n_h(l, mlp):
            return l * (NB // 2 + NM) + mlp * (NB // 2)

        def n_unit(l):
            return sum(EXPERTS[:l]) * NM

        def n_f1(l):
            return sum(FTOT[:l]) * NM

        def xb(b, lo=0, hi=C):
            return X[:, cut(b * C + lo, hi - lo)]

        block = ctx.enter_context(nc.Block())

        @block.sync
        def _(sp):
            sp.dma_start(ctmp[:, 0, :], d["cond_t"][0:C0, :]).then_inc(ld_cond, 16)
            sp.dma_start(ctmp[0:C - C0, 1, :], d["cond_t"][C0:C, :]).then_inc(ld_cond, 16)
            sp.dma_start(K[:, :], d["consts"]).then_inc(ld_cond, 16)
            sp.dma_start(lnc[:, 0:4], d["ln_col"][0:C0, :]).then_inc(ld_cond, 16)
            sp.dma_start(lnc[0:S3, 4:8], d["ln_col"][C0:XW, :]).then_inc(ld_cond, 16)
            sp.dma_start(BIG[:, 0:GC], d["ada_gate"][0:C0, :]).then_inc(ld_gw, 16)
            sp.dma_start(BIG[0:C1, GC:2 * GC], d["ada_gate"][C0:C + 1, :]).then_inc(ld_gw, 16)
            for q in range(4):
                sp.dma_start(X[:, q * 8 * C:(q + 1) * 8 * C].rearrange("p (b c) -> p b c", b=8),
                             d["x"][q * 8:(q + 1) * 8].rearrange("b t c -> t b c")).then_inc(ld_x, 16)
            A0 = 2 * GC
            sp.dma_start(BIG[:, A0:A0 + LAYERS * 4 * XW], d["ada_col"][0:C0, :]).then_inc(ld_ada, 16)
            sp.dma_start(BIG[0:C1, A0 + LAYERS * 4 * XW:A0 + 2 * LAYERS * 4 * XW], d["ada_col"][C0:C + 1, :]).then_inc(ld_ada, 16)

            def load_raw(name, n, s):
                sp.dma_start(WR[:, 0:n], d[name][0:C0, :]).then_inc(s, 16)
                for k in range(3):
                    sp.dma_start(WR3[k * C1:(k + 1) * C1, 0:n], d[name][C0:C + 1, :]).then_inc(s, 16)

            def load_wp(l):
                sp.dma_start(wp0[:, l % 2, :], d[f"wp{l}"][0:C0, :]).then_inc(ld_wp, 16)
                sp.dma_start(wp1[:, l % 2, :], d[f"wp{l}"][C0:C + 1, :]).then_inc(ld_wp, 16)

            load_raw("wqkv0", WQKV, ld_wq)
            load_wp(0)
            sp.wait_ge(s_gev, 2)
            sp.dma_start(gates_dram, gate_rows).then_inc(s_gst, 16)
            sp.wait_ge(s_gst, 16)
            for l in range(LAYERS):
                sp.wait_ge(s_split, SPLITS * (2 * l + 1))
                load_raw(f"wm{l}", WM[l], ld_wm)
                wait(sp, f2_done, n_unit(l) * MT)
                nt = EXPERTS[l] * FT
                sp.dma_start(w2[:, 0:nt, :], d[f"w2_{l}"].rearrange("(t p) c -> p t c", p=128)).then_inc(ld_w2, 16)
                if l == 1:
                    sp.dma_start(b2[:, :, :], d["b2_1"]).then_inc(ld_w2, 16)

                def sp_step(b, u):
                    wait(sp, res_done, n_batch(l, 0) + b - 3)
                    sp.dma_start(gate[:, u, :], gates_dram[cut(b, 1), 2 * l * C:(2 * l + 1) * C]
                                 .broadcast_to([128, C])).then_inc(gate_ld[u], 16)
                    sp.wait_ge(mt_ev, NB * l + b + 1)
                    for g in range(G):
                        q0 = (u % 2) * 128
                        sp.dma_start(Q[3 * HD:3 * HD + 3 * HP + 1:HP, u // 2, g, q0:q0 + 128].bitcast(F32),
                                     mT[G * g:G * g + G, u % 2, :].bitcast(F32)).then_inc(mrow, 16)

                for b in range(4):
                    sp_step(b, b)
                with sp.Fori(1, NB // 4) as i:
                    for u in range(4):
                        sp_step(4 * i + u, u)

                sp.wait_ge(s_split, SPLITS * (2 * l + 2))
                if l + 1 == LAYERS:
                    sp.dma_start(SW0, d["skew_w"][0:C0, :]).then_inc(ld_skew, 16)
                else:
                    load_raw(f"wqkv{l + 1}", WQKV, ld_wq)
                    load_wp(l + 1)

                def load_mlp_gate(m, par):
                    wait(sp, res_done, n_batch(l, 1) + MT * (m - 1))
                    for s in range(MT):
                        sp.dma_start(mgate[:, par, s * C:(s + 1) * C],
                                     gates_dram[cut(MT * m + s, 1), (2 * l + 1) * C:(2 * l + 2) * C]
                                     .broadcast_to([128, C])).then_inc(m_gate[par], 16)

                load_mlp_gate(0, 0)
                load_mlp_gate(1, 1)
                with sp.Fori(1, NM // 2) as i:
                    load_mlp_gate(2 * i, 0)
                    load_mlp_gate(2 * i + 1, 1)
            sp.wait_ge(res_done, n_batch(LAYERS, 0))
            sp.dma_start(SW1, d["skew_w"][C0:C + 1, :]).then_inc(ld_skew, 16)
            sp.wait_ge(sk_ev0, 4)
            sp.wait_ge(sk_ev1, 4)
            sp.dma_start(skew_dram, SV).then_inc(sk_st, 16)
            sp.wait_ge(sk_st, 16)
            for s in range(2):
                sp.dma_start(M[0][s * RD:(s + 1) * RD, :, :],
                             skew_dram[s * NHALF:(s + 1) * NHALF, :].rearrange("n (i j) -> i n j", i=RD)).then_inc(sk_ld, 16)
            for q in range(NM):
                sp.wait_ge(o_ev, 2 * q + 2)
                sp.dma_start(out[MT * q:MT * (q + 1)].rearrange("b t c -> t b c"),
                             X[:, MT * q * C:MT * (q + 1) * C].rearrange("p (b c) -> p b c", b=MT)).then_inc(s_out, 16)
            sp.wait_ge(s_out, 16 * NM)

        @block.vector
        def _(dve):
            V = nc.vector
            V.memset(sc1[:, :], 1.0).then_inc(s_silu, 1)
            V.memset(ones[:, :], 1.0).then_inc(s_ones, 1)
            V.memset(KBD[:, :, :, :, :].bitcast(F32), 0.0)
            V.memset(xh[:, :, :], 1.0)
            V.memset(epst[:, 0:1], EPS[0])
            V.memset(epst[:, 1:2], EPS[2]).then_inc(s_const, 1)
            dve.wait_ge(s_e, 2)
            V.tensor_scalar(ctmp[:, 2, :], ctmp[:, 2, :], 1.0, None, ALU.add)
            V.tensor_scalar(ctmp[0:C - C0, 3, :], ctmp[0:C - C0, 3, :], 1.0, None, ALU.add).then_inc(s_silu, 1)
            dve.wait_ge(s_silu, 2)
            V.reciprocal(ctmp[:, 2, :], ctmp[:, 2, :])
            V.reciprocal(ctmp[0:C - C0, 3, :], ctmp[0:C - C0, 3, :]).then_inc(s_silu, 1)
            dve.wait_ge(s_silu, 3)
            V.tensor_tensor(sc0[:, :], ctmp[:, 0, :], ctmp[:, 2, :], ALU.mult)
            V.tensor_tensor(sc1[0:C - C0, :], ctmp[0:C - C0, 1, :], ctmp[0:C - C0, 3, :], ALU.mult).then_inc(s_silu, 1)
            dve.wait_ge(ld_x, 64)

            with dve.Fori(0, NB) as b:
                V.bn_stats(st6[:, cut(b, 1), :], xb(b)).then_inc(s_st0, 1)
            for n in range(2):
                dve.wait_ge(s_gps, n + 1)
                V.tensor_copy(gate_rows[:, n * GC // 2:(n + 1) * GC // 2], PS[n][0:NB, 0:GC // 2]).then_inc(s_gev, 1)
            for l in range(LAYERS):
                dve.wait_ge(s_cps, l + 1)
                for kind in range(4):
                    for t, ps, rows in ((col0, PS[2 + 2 * (l % 2)], C0), (col1, PS[3 + 2 * (l % 2)], S3)):
                        one = float(kind % 2)
                        last = V.tensor_scalar(t[0:rows, l, kind, :], ps[0:rows, kind * NB:(kind + 1) * NB], one, None, ALU.add)
                last.then_inc(s_cev, 1)
            dve.wait_ge(s_cev, LAYERS)
            L2 = LAYERS - 1
            for ph in range(2):
                for t, rows, c in ((col0, C0, 0), (col1, S3, 4)):
                    w_, b_ = lnc[0:rows, c + 2 * ph:c + 2 * ph + 1], lnc[0:rows, c + 2 * ph + 1:c + 2 * ph + 2]
                    last = V.scalar_tensor_tensor(t[0:rows, L2, 2 * ph, :], t[0:rows, L2, 2 * ph + 1, :], b_,
                                                  t[0:rows, L2, 2 * ph, :], ALU.mult, ALU.add)
            last.then_inc(s_cln, 1)
            dve.wait_ge(s_cln, 1)
            for ph in range(2):
                for t, rows, c in ((col0, C0, 0), (col1, S3, 4)):
                    last = V.tensor_scalar(t[0:rows, L2, 2 * ph + 1, :], t[0:rows, L2, 2 * ph + 1, :],
                                           lnc[0:rows, c + 2 * ph:c + 2 * ph + 1], None, ALU.mult)
            last.then_inc(s_cln, 1)
            dve.wait_ge(s_cln, 2)

            def split(n, k):
                V.tensor_copy(Whi[:, 0:n], WR[:, 0:n]).then_inc(s_split, 1)
                dve.wait_ge(s_split, SPLITS * k + 1)
                V.tensor_tensor(Wlo[:, 0:n], WR[:, 0:n], Whi[:, 0:n].bitcast(F32), ALU.subtract).then_inc(s_split, 1)
                for q in range(SPLIT_PIECES):
                    lo, hi = q * 512, min((q + 1) * 512, n)
                    if lo < n:
                        V.tensor_copy(hshi[:, 0:hi - lo], WR3[:, lo:hi]).then_inc(s_split, 1)
                        dve.wait_ge(s_split, SPLITS * k + 3 + 2 * q)
                        V.scalar_tensor_tensor(W3[:, lo:hi], hshi[:, 0:hi - lo].bitcast(F32), K[0:S3, K_MW:K_MW + 1],
                                               WR3[:, lo:hi], ALU.mult, ALU.add).then_inc(s_split, 1)
                        dve.wait_ge(s_split, SPLITS * k + 4 + 2 * q)
                done = 2 + 2 * ((n + 511) // 512)
                if done < SPLITS:
                    V.memset(epst[:, 2:3], 0.0).then_inc(s_split, SPLITS - done)

            def rstd_all(l, mlp):
                ph = 2 * l + mlp
                eps = epst[:, l // 2:l // 2 + 1]
                dve.wait_ge(s_st0, NB) if ph == 0 else dve.wait_ge(res_done, n_batch(l, mlp))
                V.tensor_tensor(mean[:, :], st6[:, :, 1], st6[:, :, 4], ALU.add)
                V.tensor_tensor(rtmp[:, 0, :], st6[:, :, 1], st6[:, :, 4], ALU.subtract)
                V.tensor_tensor(var[:, :], st6[:, :, 2], st6[:, :, 5], ALU.add).then_inc(s_var, 1)
                dve.wait_ge(s_var, 4 * ph + 1)
                V.tensor_scalar(mean[:, :], mean[:, :], 0.5, None, ALU.mult)
                V.tensor_scalar(var[:, :], var[:, :], 1.0 / C, None, ALU.mult)
                V.tensor_tensor(rtmp[:, 0, :], rtmp[:, 0, :], rtmp[:, 0, :], ALU.mult).then_inc(s_var, 1)
                dve.wait_ge(s_var, 4 * ph + 2)
                V.scalar_tensor_tensor(var[:, :], rtmp[:, 0, :], 0.25, var[:, :], ALU.mult, ALU.add).then_inc(s_var, 2)
                dve.wait_ge(s_std, ph + 1)
                V.reciprocal(rtmp[:, 1, :], rtmp[:, 0, :])
                V.tensor_scalar(rtmp[:, 2, :], var[:, :], eps, -0.5, ALU.add, ALU.mult).then_inc(s_ln, 1)
                dve.wait_ge(s_ln, 5 * ph + 1)
                V.tensor_tensor(rtmp[:, 2, :], rtmp[:, 2, :], rtmp[:, 1, :], ALU.mult).then_inc(s_ln, 1)
                dve.wait_ge(s_ln, 5 * ph + 2)
                V.tensor_tensor(rtmp[:, 2, :], rtmp[:, 2, :], rtmp[:, 1, :], ALU.mult).then_inc(s_ln, 1)
                dve.wait_ge(s_ln, 5 * ph + 3)
                V.tensor_scalar(rtmp[:, 2, :], rtmp[:, 2, :], 1.5, None, ALU.add).then_inc(s_ln, 1)
                dve.wait_ge(s_ln, 5 * ph + 4)
                V.tensor_tensor(rstd[:, :], rtmp[:, 2, :], rtmp[:, 1, :], ALU.mult).then_inc(s_ln, 1)
                dve.wait_ge(s_ln, 5 * ph + 5)

            def normalise(b, slot):
                mu, rs = mean[:, cut(b, 1)], rstd[:, cut(b, 1)]
                V.tensor_scalar(xh[:, slot, 0:C0], xb(b, 0, C0), mu, rs, ALU.subtract, ALU.mult)
                tail = xh[:, slot, C0:XW].rearrange("p (k c) -> p k c", k=3)[:, :, 0:C1 - 1]
                src = xb(b, C0, C).rearrange("p (o c) -> p o c", o=1).broadcast_to([128, 3, C1 - 1])
                V.tensor_scalar(tail, src, mu, rs, ALU.subtract, ALU.mult).then_inc(xh_ready, 1)

            def modulate(l, mlp, b, s, p0, p1, q0):
                sh, scl = 2 * mlp, 2 * mlp + 1
                V.tensor_scalar(hf[:, s * 128:(s + 1) * 128], p0[:, s * 128:(s + 1) * 128],
                                col0[:, l, scl, cut(b, 1)], col0[:, l, sh, cut(b, 1)], ALU.mult, ALU.add)
                return V.tensor_scalar(hs[:, s * 128:(s + 1) * 128], p1[0:S3, q0 + s * 128:q0 + (s + 1) * 128],
                                       col1[:, l, scl, cut(b, 1)], col1[:, l, sh, cut(b, 1)], ALU.mult, ALU.add)

            def low_parts(par, n):
                V.tensor_tensor(hlo[:, par, 0:n], hf[:, 0:n], hhi[:, par, 0:n].bitcast(F32), ALU.subtract)
                V.scalar_tensor_tensor(h3[:, par, 0:n], hshi[:, 0:n].bitcast(F32), K[0:S3, K_MH:K_MH + 1], hs[:, 0:n],
                                       ALU.mult, ALU.add).then_inc(h_ready, 1)

            def residual(n, b, y_ps, g):
                V.tensor_tensor(ytmp[:, :], y_ps, g, ALU.mult).then_inc(y_read, 1)
                dve.wait_ge(y_read, n + 1)
                V.tensor_tensor(xb(b), xb(b), ytmp[:, :], ALU.add).then_inc(x_new, 1)
                dve.wait_ge(x_new, n + 1)
                dve.wait_ge(s_const, 1)
                V.bn_stats(st6[:, cut(b, 1), :], xb(b)).then_inc(res_done, 1)

            for l in range(LAYERS):
                dve.wait_ge(ld_wq, 64 * (l + 1))
                if l == 0:
                    dve.wait_ge(s_cps, LAYERS)
                split(WQKV, 2 * l)
                rstd_all(l, 0)
                if l:
                    dve.wait_ge(f2_done, n_unit(l) * MT)
                V.memset(BIG[:, 0:2048], 0.0).then_inc(va_set, 1)
                dve.wait_ge(va_set, 3 * l + 1)
                V.memset(VA[:, :, :, HD:HD + 1], 1.0).then_inc(va_set, 1)
                V.memset(oq[:, :, C:C + 1], 1.0).then_inc(va_set, 1)

                def h_first(P, u2):
                    dve.wait_ge(xt_done, n_h(l, 0) + P + 1)
                    wait(dve, h_ready, n_h(l, 0) + P)
                    modulate(l, 0, 2 * P, 0, PS[5], PS[5], 256)
                    modulate(l, 0, 2 * P + 1, 1, PS[5], PS[5], 256).then_inc(hf_ready, 1)

                def h_second(P, par):
                    dve.wait_ge(hhi_ready, n_h(l, 0) + P + 1)
                    wait(dve, v_ps, NB // 2 * l + P - 1)
                    low_parts(par, 256)

                def qk_stack(pn, par, j):
                    n = 4 * pn + j
                    dve.wait_ge(qk_hi, n + 1)
                    m = K[:, (K_MQ, K_MK)[j // 2]:(K_MQ, K_MK)[j // 2] + 1]
                    if j < 2:
                        o = Q[:, par, 2 * j:2 * j + 2, :].rearrange("p g n -> p (g n)")
                    else:
                        o = kst[:, :]
                        wait(dve, kbd_a, 2 * pn + j - 2)
                        wait(dve, kbd_v, 2 * pn + j - 2)
                    V.scalar_tensor_tensor(o, qkhi[:, :].bitcast(F32), m, PS[4][:, :], ALU.mult, ALU.add).then_inc(qk_lo, 1)
                    if j >= 2:
                        dve.wait_ge(qk_lo, n + 1)
                        for r in (2, 3):
                            rows = slice(HP * r, HP * (r + 1))
                            last = V.tensor_copy(KBD[rows, par, 2 * j - 4:2 * j - 2, r, :],
                                                 kst[rows, :].rearrange("p (g n) -> p g n", g=2))
                        last.then_inc(kbd_v, 1)

                def values(P, par):
                    dve.wait_ge(v_ps, NB // 2 * l + P + 1)
                    for s in range(2):
                        last = V.tensor_copy(VA[:, 2 * par + s, :, 0:HD],
                                             PS[5][:, s * C:(s + 1) * C].rearrange("p (h w) -> p h w", h=NH))
                    last.then_inc(v_ev, 1)

                def row_max(b, u, g):
                    n = 4 * (NB * l + b) + g
                    dve.wait_ge(s1_done, n + 1)
                    V.tensor_reduce(nmax[:, u % 2, HG * g:HG * g + HG], PS[g % 2][:, :].rearrange("p (r k) -> p r k", r=HG),
                                    AX.X, ALU.max, negate=True).then_inc(max_done, 1)

                def normalise_out(b, u):
                    n = NB * l + b
                    dve.wait_ge(otr_done, n + 1)
                    ps = PS[7][:, :].rearrange("p (h w) -> p h w", w=HP)
                    V.reciprocal(rsum[:, u % 2, :], ps[:, :, HD]).then_inc(rs_done, 1)
                    dve.wait_ge(rs_done, n + 1)
                    V.tensor_tensor(oq[:, u % 2, 0:C].rearrange("p (h w) -> p h w", h=NH), ps[:, :, 0:HD],
                                    rsum[:, u % 2, :].rearrange("p (h o) -> p h o", o=1).broadcast_to([128, NH, HD]),
                                    ALU.mult).then_inc(norm_done, 1)

                def step(t, u, i=None):
                    static = i is None
                    P, par, odd = (t // 2 if static else 2 * i + u // 2), u // 2, u % 2
                    pn = NB // 2 * l + P + 1
                    live = not static or t < NB
                    nxt = not static or P + 1 < NB // 2
                    nxt2 = not static or P + 2 < NB // 2
                    if live and not odd and not (static and t == 0):
                        values(P, par)
                    if not static or t + 4 < NB:
                        normalise(t + 4, u)
                    if live:
                        row_max(t, u, 0)
                        if odd and nxt:
                            qk_stack(pn, 1 - par, 1)
                    if not static or t >= 2:
                        normalise_out(t - 2, (u + 2) % 4)
                    if live:
                        row_max(t, u, 1)
                        if odd and nxt2:
                            h_first(P + 2, 0)
                        row_max(t, u, 2)
                        if odd and nxt:
                            qk_stack(pn, 1 - par, 2)
                        if odd and nxt2:
                            h_second(P + 2, par)
                        row_max(t, u, 3)
                    if not static or t >= 2:
                        attn_residual_at(t - 2, (u + 2) % 4, None if static else (i - 1 if u < 2 else i))
                    if live and nxt:
                        qk_stack(pn, 1 - par, 3 if odd else 0)

                def attn_residual_at(b, u, gi):
                    dve.wait_ge(y_done, NB * l + b + 1)
                    dve.wait_ge(gate_ld[u], 16 * (NB // 4 * l + b // 4 + 1) if gi is None else 16 * (gi + NB // 4 * l + 1))
                    residual(n_batch(l, 0) + b, b, PS[7][:, 0:C], gate[:, u, :])

                for b in range(4):
                    normalise(b, b)
                h_first(0, 0)
                h_second(0, 0)
                for j in range(4):
                    qk_stack(NB // 2 * l, 0, j)
                values(0, 0)
                h_first(1, 0)
                h_second(1, 1)
                for t in range(4):
                    step(t, t)
                with dve.Fori(1, NB // 4 - 1) as i:
                    for u in range(4):
                        step(4 * i + u, u, i)
                for t in range(NB - 4, NB + 2):
                    step(t, t % 4)

                dve.wait_ge(ld_wm, 64 * (l + 1))
                split(WM[l], 2 * l + 1)
                dve.wait_ge(res_done, n_batch(l, 1))
                rstd_all(l, 1)
                if l != 1:
                    dve.wait_ge(y_done, NB * (l + 1))
                    V.memset(hm[64:65, 4, :], 1.0)
                    V.memset(hm[64:65, 9, :], 1.0).then_inc(hm_ones, 1)

                def mlp_rows(m, par):
                    for s in range(MT):
                        normalise(MT * m + s, MT * par + s)

                def mlp_h(m, par):
                    dve.wait_ge(xt_done, n_h(l, 1) + m + 1)
                    wait(dve, h_ready, n_h(l, 1) + m)
                    for s in range(MT):
                        last = modulate(l, 1, MT * m + s, s, PS[5], PS[4], 0)
                    last.then_inc(hf_ready, 1)
                    dve.wait_ge(hhi_ready, n_h(l, 1) + m + 1)
                    wait(dve, f1_done, n_f1(l) + FTOT[l] * (m - 1))
                    low_parts(par, 512)

                def router(m):
                    n0 = 12 * m
                    lg, gt, eq, rk, r0, r1, t0, t1, m0, m1, df, th, cw = (
                        rt[:, 0:16], rt[:, 16:80], rt[:, 80:144], rt[:, 144:160], rt[:, 160:176], rt[:, 176:192],
                        rt[:, 192:208], rt[:, 208:224], rt[:, 224:228], rt[:, 228:232], rt[:, 232:236], rt[:, 236:240],
                        rt[:, 240:256])

                    def q4(a):
                        return a.rearrange("p (s e j) -> p s e j", s=MT, e=NE)

                    lj = lg.rearrange("p (s o j) -> p s o j", s=MT, o=1).broadcast_to([128, MT, NE, NE])
                    le = lg.rearrange("p (s e o) -> p s e o", s=MT, o=1).broadcast_to([128, MT, NE, NE])
                    low = K[:, K_LOW:K_N].rearrange("p (o e j) -> p o e j", o=1, e=NE).broadcast_to([128, MT, NE, NE])
                    dve.wait_ge(g_ps, m + 1)
                    V.tensor_copy(lg, PS[2][:, 0:16]).then_inc(g_steps, 1)
                    dve.wait_ge(g_steps, n0 + 1)
                    V.tensor_tensor(q4(gt), lj, le, ALU.is_gt)
                    V.tensor_tensor(q4(eq), lj, le, ALU.is_equal).then_inc(g_steps, 1)
                    dve.wait_ge(g_steps, n0 + 2)
                    V.tensor_tensor(q4(eq), q4(eq), low, ALU.mult).then_inc(g_steps, 1)
                    dve.wait_ge(g_steps, n0 + 3)
                    V.tensor_tensor(gt, gt, eq, ALU.add).then_inc(g_steps, 1)
                    dve.wait_ge(g_steps, n0 + 4)
                    V.tensor_reduce(rk, gt.rearrange("p (a j) -> p a j", j=NE), AX.X, ALU.add).then_inc(g_steps, 1)
                    dve.wait_ge(g_steps, n0 + 5)
                    V.tensor_scalar(r0, rk, 0.0, 0.5, ALU.is_equal, ALU.mult)
                    V.tensor_scalar(r1, rk, 1.0, 0.5, ALU.is_equal, ALU.mult).then_inc(g_steps, 1)
                    dve.wait_ge(g_steps, n0 + 6)
                    V.tensor_tensor(t0, r0, lg, ALU.mult)
                    V.tensor_tensor(t1, r1, lg, ALU.mult).then_inc(g_steps, 1)
                    dve.wait_ge(g_steps, n0 + 7)
                    V.tensor_reduce(m0, t0.rearrange("p (s e) -> p s e", s=MT), AX.X, ALU.add)
                    V.tensor_reduce(m1, t1.rearrange("p (s e) -> p s e", s=MT), AX.X, ALU.add).then_inc(g_steps, 1)
                    dve.wait_ge(g_steps, n0 + 8)
                    V.tensor_tensor(df, m0, m1, ALU.subtract).then_inc(g_steps, 1)
                    V.tensor_tensor(t0, r0, r1, ALU.subtract)
                    V.tensor_tensor(t1, r0, r1, ALU.add).then_inc(g_steps, 1)
                    dve.wait_ge(g_th, m + 1)
                    dve.wait_ge(g_steps, n0 + 10)
                    thb = th.rearrange("p (s o) -> p s o", o=1).broadcast_to([128, MT, NE])
                    V.tensor_tensor(t0.rearrange("p (s e) -> p s e", s=MT), t0.rearrange("p (s e) -> p s e", s=MT), thb,
                                    ALU.mult).then_inc(g_steps, 1)
                    dve.wait_ge(g_steps, n0 + 11)
                    V.tensor_tensor(cw, t0, t1, ALU.add).then_inc(g_steps, 1)
                    dve.wait_ge(g_steps, n0 + 12)

                cw = rt[:, 240:256]

                def mlp_out(m, par, gr):
                    for e in range(EXPERTS[l]):
                        for s in range(MT):
                            n = (n_unit(l) + EXPERTS[l] * m + e) * MT + s
                            ps = PS[6 + s % 2][:, 0:C]
                            dve.wait_ge(f2_done, n + 1)
                            a = acc[:, s * C:(s + 1) * C]
                            if l != 1:
                                V.tensor_copy(a, ps).then_inc(acc_done, 1)
                            elif e == 0:
                                V.tensor_scalar(a, ps, cw[:, s * NE:s * NE + 1], None, ALU.mult).then_inc(acc_done, 1)
                            else:
                                V.scalar_tensor_tensor(a, ps, cw[:, s * NE + e:s * NE + e + 1], a, ALU.mult, ALU.add).then_inc(acc_done, 1)
                    dve.wait_ge(m_gate[par], 64 * (NM // 2 * l + gr + 1))
                    last_n = (n_unit(l) + EXPERTS[l] * (m + 1)) * MT
                    dve.wait_ge(acc_done, last_n)
                    for s in range(MT):
                        residual(n_batch(l, 1) + MT * m + s, MT * m + s, acc[:, s * C:(s + 1) * C],
                                 mgate[:, par, s * C:(s + 1) * C])

                mlp_rows(0, 0)
                mlp_h(0, 0)
                mlp_rows(1, 1)

                def mlp_step(m, par, gr, more1, more2):
                    if l == 1:
                        router(m)
                    if more1:
                        mlp_h(m + 1, 1 - par)
                    if more2:
                        mlp_rows(m + 2, par)
                    mlp_out(m, par, gr)

                with dve.Fori(0, NM // 2 - 1) as i:
                    mlp_step(2 * i, 0, i, True, True)
                    mlp_step(2 * i + 1, 1, i, True, True)
                mlp_step(NM - 2, 0, NM // 2 - 1, True, False)
                mlp_step(NM - 1, 1, NM // 2 - 1, False, False)
                dve.wait_ge(res_done, n_batch(l, 1) + NB)
            for c in range(0, 8, 2):
                dve.wait_ge(sk_ps, c + 1)
                V.tensor_copy(SV[:, c * 512:(c + 1) * 512], PS[c][0:NB, :]).then_inc(sk_ev0, 1)
            rev = [0]

            def stepped(ins):
                rev[0] += 1
                ins.then_inc(r_ev, 1)
                return rev[0]

            def flat(m):
                return m.rearrange("p n j -> p (n j)")

            def quarter(m, k):
                s, h = k // 2, k % 2
                return flat(m)[s * RD:(s + 1) * RD, h * 512:(h + 1) * 512]

            def bank(b0, k):
                return PS[b0 + k][(k // 2) * RD:(k // 2 + 1) * RD, :]

            RAW, A, A2, A3, A4, BE, BO, EE, EO = M[0], M[1], M[2], M[3], M[4], M[5], M[0], M[6], M[7]
            sgn = K[:, K_SGN:K_SGN + RD].rearrange("p (o j) -> p o j", o=1).broadcast_to([128, NHALF, RD])
            dve.wait_ge(sk_ld, 32)
            stepped(V.scalar_tensor_tensor(A, RAW, 2.0 ** -SQUARINGS, sgn, ALU.mult, ALU.mult))
            dve.wait_ge(r_ps, 1)
            for k in range(4):
                stepped(V.tensor_scalar(quarter(A2, k), bank(0, k), -1.0, None, ALU.mult))
            dve.wait_ge(r_ev, 5)
            stepped(V.tensor_scalar(flat(BE), flat(A2), 1 / 720, None, ALU.mult))
            dve.wait_ge(r_ps, 2)
            for k in range(4):
                stepped(V.tensor_scalar(quarter(A3, k), bank(4, k), -1.0, None, ALU.mult))
            dve.wait_ge(r_ps, 3)
            for k in range(4):
                stepped(V.tensor_copy(quarter(A4, k), bank(0, k)))
            dve.wait_ge(r_ev, 14)
            stepped(V.scalar_tensor_tensor(flat(BE), flat(A4), 1 / 40320, flat(BE), ALU.mult, ALU.add))
            stepped(V.tensor_scalar(flat(BO), flat(A), 1 / 120, None, ALU.mult))
            dve.wait_ge(r_ev, 16)
            stepped(V.scalar_tensor_tensor(flat(BO), flat(A3), 1 / 5040, flat(BO), ALU.mult, ALU.add))
            stepped(V.tensor_scalar(flat(EE), flat(A2), 0.5, None, ALU.mult))
            dve.wait_ge(r_ev, 18)
            stepped(V.scalar_tensor_tensor(flat(EE), flat(A4), 1 / 24, flat(EE), ALU.mult, ALU.add))
            stepped(V.scalar_tensor_tensor(flat(EO), flat(A3), 1 / 6, flat(A), ALU.mult, ALU.add))
            dve.wait_ge(r_ev, 20)
            dve.wait_ge(r_ps, 4)
            for k in range(4):
                stepped(V.tensor_tensor(quarter(EE, k), quarter(EE, k), bank(0, k), ALU.add))
            dve.wait_ge(r_ps, 5)
            for k in range(4):
                stepped(V.tensor_tensor(quarter(EO, k), quarter(EO, k), bank(4, k), ALU.add))
            dve.wait_ge(r_ev, 28)
            stepped(V.tensor_tensor(flat(FM[0]), flat(EE), flat(EO), ALU.add))
            stepped(V.tensor_tensor(flat(FM[1]), flat(EE), flat(EO), ALU.subtract))
            for q in range(SQUARINGS):
                old, new = (FM[0:2], FM[2:4]) if q % 2 == 0 else (FM[2:4], FM[0:2])
                dve.wait_ge(r_ev, 30 + 8 * q)
                for w in range(2 if q + 1 < SQUARINGS else 1):
                    dve.wait_ge(r_ps, 6 + 2 * q + w)
                    for k in range(4):
                        stepped(V.scalar_tensor_tensor(quarter(new[w], k), quarter(old[w], k), 2.0, bank(4 * w, k),
                                                       ALU.mult, ALU.add))
            dve.wait_ge(qr_done, 1)
            for k in range(2):
                last = V.tensor_copy(UD[:, :, k * RD:(k + 1) * RD], QU[:, :, :])
            last.then_inc(u_dup, 1)
            dve.wait_ge(u_ps, 1)
            V.tensor_copy(UT[:, :], PS[7][:, 0:C]).then_inc(u_ev, 1)

            def z_copy(q):
                s = q // (NM // 2)
                dve.wait_ge(z_ps, q + 1)
                wait(dve, yy_ps, q - 1)
                V.tensor_copy(zs[s * RD:(s + 1) * RD, (q % 2) * 512:(q % 2 + 1) * 512], PS[4][s * RD:(s + 1) * RD, :])\
                    .then_inc(z_ev, 1)

            def rotated(q):
                for h in range(2):
                    dve.wait_ge(o_ps, 2 * q + h + 1)
                    x2 = X[:, (MT * q + 2 * h) * C:(MT * q + 2 * h + 2) * C]
                    V.tensor_tensor(x2, x2, PS[6 + h][:, 0:2 * C], ALU.add).then_inc(o_ev, 1)

            for q in range(NM):
                z_copy(q)
                if q:
                    rotated(q - 1)
            rotated(NM - 1)

        @block.scalar
        def _(act):
            S = nc.scalar
            act.wait_ge(ld_cond, 80)
            S.activation(ctmp[:, 2, :], ctmp[:, 0, :], ACT.Exp, scale=-1.0).then_inc(s_e, 1)
            S.activation(ctmp[0:C - C0, 3, :], ctmp[0:C - C0, 1, :], ACT.Exp, scale=-1.0).then_inc(s_e, 1)
            act.wait_ge(s_const, 1)

            def root(l, mlp):
                act.wait_ge(s_var, 4 * (2 * l + mlp + 1))
                S.activation(rtmp[:, 0, :], var[:, :], ACT.Sqrt, bias=epst[:, l // 2:l // 2 + 1]).then_inc(s_std, 1)

            for l in range(LAYERS):
                root(l, 0)

                def h_high(P, par):
                    act.wait_ge(hf_ready, n_h(l, 0) + P + 1)
                    wait(act, h_ready, n_h(l, 0) + P)
                    wait(act, v_ps, NB // 2 * l + P - 1)
                    S.activation(hhi[:, par, 0:256], hf[:, 0:256], ACT.Copy)
                    S.activation(hshi[:, 0:256], hs[:, 0:256], ACT.Copy).then_inc(hhi_ready, 1)

                def qk_high(n):
                    act.wait_ge(qk_ps, n + 1)
                    wait(act, qk_lo, n)
                    S.activation(qkhi[:, :], PS[4][:, :], ACT.Copy).then_inc(qk_hi, 1)

                def k_place(pn, par, j):
                    act.wait_ge(qk_lo, 4 * pn + j + 1)
                    for r in (0, 1):
                        rows = slice(HP * r, HP * (r + 1))
                        last = S.activation(KBD[rows, par, 2 * j - 4:2 * j - 2, r, :],
                                            kst[rows, :].rearrange("p (g n) -> p g n", g=2), ACT.Copy)
                    last.then_inc(kbd_a, 1)

                def exps(b, u, g):
                    n = 4 * (NB * l + b) + g
                    act.wait_ge(s2_done, n + 1)
                    wait(act, pv_done, NB * l + b - 1)
                    S.activation(PT[:, u % 2, g, :], PS[2 + g % 2][:, :], ACT.Exp, scale=float(HD) ** -0.5).then_inc(exp_done, 1)

                def out_copy(b, u):
                    n = NB * l + b
                    act.wait_ge(pv_done, n + 1)
                    wait(act, otr_done, n - 1)
                    S.activation(OTs[:, u % 2, :], PS[6][:, :], ACT.Copy).then_inc(ot_ev, 1)

                def oT_copy(b, u):
                    n = NB * l + b
                    act.wait_ge(ot2_done, n + 1)
                    wait(act, y_done, n - 1)
                    S.activation(oT[:, u % 2, 0:128], PS[7][:, 0:128], ACT.Copy)
                    S.activation(oT[0:C1, u % 2, 128:256], PS[7][0:C1, 128:256], ACT.Copy).then_inc(oT_ev, 1)

                def max_copy(b, u):
                    n = NB * l + b
                    act.wait_ge(mt_done, n + 1)
                    wait(act, mrow, 64 * (n - 1))
                    S.activation(mT[:, u % 2, :], PS[5][0:NH, 0:128], ACT.Copy).then_inc(mt_ev, 1)

                def step(t, u, i=None):
                    static = i is None
                    P, par, odd = (t // 2 if static else 2 * i + u // 2), u // 2, u % 2
                    pair_n = NB // 2 * l + P + 1
                    base = 4 * pair_n
                    live = not static or t < NB
                    nxt = not static or P + 1 < NB // 2
                    before = not static or 1 <= t <= NB
                    tail = not static or t >= 2
                    if tail:
                        out_copy(t - 2, u)
                    if before:
                        exps(t - 1, u + 1, 0)
                    if live and odd and nxt:
                        qk_high(base + 1)
                    if before:
                        exps(t - 1, u + 1, 1)
                    if live and odd and (not static or P + 2 < NB // 2):
                        h_high(P + 2, par)
                    if before:
                        exps(t - 1, u + 1, 2)
                    if tail:
                        oT_copy(t - 2, u)
                    if live and odd and nxt:
                        qk_high(base + 2)
                    if before:
                        exps(t - 1, u + 1, 3)
                    if live and odd and nxt:
                        k_place(pair_n, 1 - par, 2)
                    if live and nxt:
                        qk_high(base + (3 if odd else 0))
                    if live:
                        max_copy(t, u)
                    if live and odd and nxt:
                        k_place(pair_n, 1 - par, 3)

                h_high(0, 0)
                for j in range(4):
                    qk_high(4 * (NB // 2) * l + j)
                    if j >= 2:
                        k_place(NB // 2 * l, 0, j)
                h_high(1, 1)
                for t in range(4):
                    step(t, t)
                with act.Fori(1, NB // 4 - 1) as i:
                    for u in range(4):
                        step(4 * i + u, u, i)
                for t in range(NB - 4, NB + 2):
                    step(t, t % 4)

                root(l, 1)
                gelu = ACT.Gelu if l == 2 else ACT.Gelu_apprx_tanh

                def mlp_high(m, par):
                    act.wait_ge(hf_ready, n_h(l, 1) + m + 1)
                    wait(act, h_ready, n_h(l, 1) + m)
                    wait(act, f1_done, n_f1(l) + FTOT[l] * (m - 1))
                    S.activation(hhi[:, par, :], hf[:, :], ACT.Copy)
                    S.activation(hshi[:, :], hs[:, :], ACT.Copy).then_inc(hhi_ready, 1)

                def gelus(m, par, e):
                    j0 = sum(FTILES[l][:e])
                    for j in range(j0, j0 + FTILES[l][e]):
                        n = n_f1(l) + FTOT[l] * m + j
                        act.wait_ge(f1_done, n + 1)
                        wait(act, f2_done, (n_unit(l) + (4 * m if l == 1 else m - 1)) * MT)
                        rows = 64 if l != 1 and j == 4 else 128
                        slot = j if l == 1 else 5 * par + j
                        S.activation(hm[0:rows, slot, :], PS[(par * FTOT[l] + j) % 2][0:rows, :], gelu).then_inc(gelu_done, 1)

                def mlp_step(m, par, more):
                    gelus(m, par, 0)
                    if l == 1:
                        act.wait_ge(g_steps, 12 * m + 10)
                        S.activation(rt[:, 236:240], rt[:, 232:236], ACT.Tanh).then_inc(g_th, 1)
                    if more:
                        mlp_high(m + 1, 1 - par)
                    for e in range(1, EXPERTS[l]):
                        gelus(m, par, e)

                mlp_high(0, 0)
                if l == 0:
                    mlp_step(0, 0, True)
                    mlp_step(1, 1, True)
                with act.Fori(int(l == 0), NM // 2 - 1) as i:
                    mlp_step(2 * i, 0, True)
                    mlp_step(2 * i + 1, 1, True)
                mlp_step(NM - 2, 0, True)
                mlp_step(NM - 1, 1, False)
            for c in range(1, 8, 2):
                act.wait_ge(sk_ps, c + 1)
                S.activation(SV[:, c * 512:(c + 1) * 512], PS[c][0:NB, :], ACT.Copy).then_inc(sk_ev1, 1)

            def x_copy(q):
                act.wait_ge(t_ps, q + 1)
                wait(act, z_ps, q - 1)
                at = (q % 2) * 512
                S.activation(xT0[:, at:at + 512], PS[2 * (q % 2)][:, :], ACT.Copy)
                S.activation(xT1[:, at:at + 512], PS[2 * (q % 2) + 1][0:C - C0, :], ACT.Copy).then_inc(t_ev, 1)

            act.wait_ge(u_ps, 1)
            x_copy(0)
            for q in range(NM):
                if q + 1 < NM:
                    x_copy(q + 1)
                s = q // (NM // 2)
                act.wait_ge(yy_ps, q + 1)
                wait(act, o_ps, 2 * (q - 1))
                S.activation(ys[s * RD:(s + 1) * RD, (q % 2) * 512:(q % 2 + 1) * 512], PS[5][s * RD:(s + 1) * RD, :],
                             ACT.Copy).then_inc(yy_ev, 1)

        @block.tensor
        def _(pe):
            mm = nc.tensor.matmul
            pe.wait_ge(s_silu, 4)
            pe.wait_ge(ld_gw, 32)
            for n in range(2):
                lo, hi = n * GC // 2, (n + 1) * GC // 2
                mm(PS[n][0:NB, 0:GC // 2], sc0[:, :], BIG[:, lo:hi], start=True, stop=False)
                mm(PS[n][0:NB, 0:GC // 2], sc1[:, :], BIG[0:C1, GC + lo:GC + hi], start=False, stop=True).then_inc(s_gps, 1)
            pe.wait_ge(ld_ada, 32)
            A0, A1 = 2 * GC, 2 * GC + LAYERS * 4 * XW
            for l in range(LAYERS):
                if l == 2:
                    pe.wait_ge(s_cev, 1)
                for kind in range(4):
                    at = (4 * l + kind) * XW
                    for ps, off, rows in ((PS[2 + 2 * (l % 2)], 0, C0), (PS[3 + 2 * (l % 2)], C0, S3)):
                        o = ps[0:rows, kind * NB:(kind + 1) * NB]
                        mm(o, BIG[:, A0 + at + off:A0 + at + off + rows], sc0[:, :], start=True, stop=False)
                        last = mm(o, BIG[0:C1, A1 + at + off:A1 + at + off + rows], sc1[:, :], start=False, stop=True)
                last.then_inc(s_cps, 1)

            def split_product(o, w, h0, par, n0, n, weights_moving=False):
                pairs = ((Whi[:, w], hhi[:, par, n0:n0 + n]), (Wlo[:, w], hhi[:, par, n0:n0 + n]),
                         (Whi[:, w], hlo[:, par, n0:n0 + n]), (W3[:, w], h3[:, par, n0:n0 + n]))
                for k, (a, b) in enumerate(pairs):
                    if weights_moving:
                        a, b = b, a
                    last = mm(o, a, b, start=(k == 0), stop=(k == 3))
                return last

            for l in range(LAYERS):
                pe.wait_ge(s_split, SPLITS * (2 * l + 1))
                pe.wait_ge(ld_wp, 32 * (l + 1))
                if l == 0:
                    pe.wait_ge(s_cev, LAYERS)
                else:
                    pe.wait_ge(res_done, n_batch(l, 0))

                def turn(P, par):
                    pe.wait_ge(xh_ready, n_batch(l, 0) + 2 * P + 2)
                    for s in range(2):
                        slot = 2 * par + s
                        nc.tensor.transpose(PS[5][:, s * 128:(s + 1) * 128], xh[:, slot, 0:C0], ident)
                        last = nc.tensor.transpose(PS[5][0:S3, 256 + s * 128:256 + (s + 1) * 128], xh[:, slot, C0:XW], ident)
                    last.then_inc(xt_done, 1)

                def qk_product(P, par, j):
                    n = 4 * (NB // 2 * l + P) + j
                    if j == 0:
                        pe.wait_ge(h_ready, n_h(l, 0) + P + 1)
                    wait(pe, qk_lo, n)
                    for gg in range(2):
                        g = 2 * (j % 2) + gg
                        w0 = (j // 2) * G * 128 + g * 128
                        last = split_product(PS[4][:, gg * 256:(gg + 1) * 256], slice(w0, w0 + 128), None, par, 0, 256)
                    last.then_inc(qk_ps, 1)

                def v_product(P, par):
                    for s in range(2):
                        last = split_product(PS[5][:, s * C:(s + 1) * C], slice(2 * G * 128, WQKV), None, par, s * 128, 128,
                                             weights_moving=True)
                    last.then_inc(v_ps, 1)

                def s1(b, u, g):
                    n = 4 * (NB * l + b) + g
                    wait(pe, max_done, n - 1)
                    q0 = (u % 2) * 128
                    mm(PS[g % 2][:, :], Q[:, u // 2, g, q0:q0 + 128], KBD[:, u // 2, g, :, q0:q0 + 128],
                       start=True, stop=True).then_inc(s1_done, 1)

                def s2(b, u, g):
                    n = 4 * (NB * l + b) + g
                    wait(pe, exp_done, n - 1)
                    if g == 0:
                        pe.wait_ge(mrow, 64 * (NB * l + b + 1))
                    q0 = (u % 2) * 128
                    for r in range(HG):
                        last = mm(PS[2 + g % 2][:, r * 128:(r + 1) * 128], KBD[:, u // 2, g, r, q0:q0 + 128],
                                  Q[:, u // 2, g, q0:q0 + 128], start=True, stop=True)
                    last.then_inc(s2_done, 1)

                def pv(b, u, g, vn):
                    n = NB * l + b
                    if g == 0:
                        wait(pe, ot_ev, n)
                        pe.wait_ge(v_ev, vn)
                    pe.wait_ge(exp_done, 4 * n + g + 1)
                    for r in range(HG):
                        last = mm(PS[6][HP * r:HP * (r + 1), g * 128:(g + 1) * 128], VA[:, u, G * g + r, :],
                                  PT[:, u % 2, g, r * 128:(r + 1) * 128], start=True, stop=True)
                    if g == G - 1:
                        last.then_inc(pv_done, 1)

                def max_turn(b, u):
                    pe.wait_ge(max_done, 4 * (NB * l + b + 1))
                    nc.tensor.transpose(PS[5][0:NH, 0:128], nmax[:, u % 2, :], ident).then_inc(mt_done, 1)

                def out_back(b, u):
                    n = NB * l + b
                    pe.wait_ge(ot_ev, n + 1)
                    wait(pe, y_read, n_batch(l, 0) + b)
                    for g in range(G):
                        last = nc.tensor.transpose(PS[7][:, g * 128:(g + 1) * 128], OTs[:, u % 2, g * 128:(g + 1) * 128], ident)
                    last.then_inc(otr_done, 1)

                def out_turn(b, u):
                    pe.wait_ge(norm_done, NB * l + b + 1)
                    nc.tensor.transpose(PS[7][:, 0:128], oq[:, u % 2, 0:C0], ident)
                    nc.tensor.transpose(PS[7][0:C1, 128:256], oq[:, u % 2, C0:C + 1], ident).then_inc(ot2_done, 1)

                def project(b, u):
                    pe.wait_ge(oT_ev, NB * l + b + 1)
                    mm(PS[7][:, 0:C], oT[:, u % 2, 0:128], wp0[:, l % 2, :], start=True, stop=False)
                    mm(PS[7][:, 0:C], oT[0:C1, u % 2, 128:256], wp1[:, l % 2, :], start=False, stop=True).then_inc(y_done, 1)

                def step(t, u, i=None):
                    static = i is None
                    P, par, odd = (t // 2 if static else 2 * i + u // 2), u // 2, u % 2
                    live = not static or t < NB
                    nxt = not static or P + 1 < NB // 2
                    nxt2 = not static or P + 2 < NB // 2
                    before = not static or 1 <= t <= NB
                    tail = not static or t >= 2
                    u1, u2 = (u + 3) % 4, (u + 2) % 4
                    if live and not odd:
                        pe.wait_ge(kbd_a, 2 * (NB // 2 * l + P + 1))
                        pe.wait_ge(kbd_v, 2 * (NB // 2 * l + P + 1))
                    if live:
                        s1(t, u, 0)
                    if before:
                        s2(t - 1, u1, 0)
                    if live and odd and nxt:
                        qk_product(P + 1, 1 - par, 1)
                    if tail:
                        out_back(t - 2, u2)
                    if live:
                        s1(t, u, 1)
                    if before:
                        s2(t - 1, u1, 1)
                    if live and odd and nxt2:
                        pe.wait_ge(mt_ev, NB * l + t)
                        turn(P + 2, par)
                    if live:
                        s1(t, u, 2)
                    if before:
                        s2(t - 1, u1, 2)
                    if live and odd and nxt:
                        qk_product(P + 1, 1 - par, 2)
                    if tail:
                        out_turn(t - 2, u2)
                    if live:
                        s1(t, u, 3)
                    if before:
                        s2(t - 1, u1, 3)
                    if tail:
                        project(t - 2, u2)
                    if live and nxt:
                        qk_product(P + 1, 1 - par, 3 if odd else 0)
                    vn = None if not before else (NB // 2 * l + ((t - 1) // 2 if static else (2 * i + u // 2 - (0 if odd else 1))) + 1)
                    if before:
                        pv(t - 1, u1, 0, vn)
                        pv(t - 1, u1, 1, vn)
                    if live:
                        pe.wait_ge(v_ev, NB // 2 * l + P + 1)
                        if odd and nxt2:
                            pe.wait_ge(hf_ready, n_h(l, 0) + P + 3)
                        max_turn(t, u)
                    if before:
                        pv(t - 1, u1, 2, vn)
                        pv(t - 1, u1, 3, vn)
                    if live and odd and nxt:
                        pe.wait_ge(mt_ev, NB * l + t + 1)
                        v_product(P + 1, 1 - par)

                turn(0, 0)
                for j in range(4):
                    qk_product(0, 0, j)
                v_product(0, 0)
                pe.wait_ge(v_ev, NB // 2 * l + 1)
                turn(1, 1)
                pe.wait_ge(va_set, 3 * (l + 1))
                pe.wait_ge(hf_ready, n_h(l, 0) + 2)
                for t in range(4):
                    step(t, t)
                with pe.Fori(1, NB // 4 - 1) as i:
                    for u in range(4):
                        step(4 * i + u, u, i)
                for t in range(NB - 4, NB + 2):
                    step(t, t % 4)

                pe.wait_ge(s_split, SPLITS * (2 * l + 2))
                pe.wait_ge(ld_w2, (16, 48, 64)[l])
                pe.wait_ge(res_done, n_batch(l, 1))
                if l != 1:
                    pe.wait_ge(hm_ones, 1 if l == 0 else 2)

                def turn_rows(m, par):
                    pe.wait_ge(xh_ready, n_batch(l, 1) + MT * (m + 1))
                    wait(pe, hf_ready, n_h(l, 1) + m)
                    for s in range(MT):
                        slot = MT * par + s
                        nc.tensor.transpose(PS[5][:, s * 128:(s + 1) * 128], xh[:, slot, 0:C0], ident)
                        last = nc.tensor.transpose(PS[4][0:S3, s * 128:(s + 1) * 128], xh[:, slot, C0:XW], ident)
                    last.then_inc(xt_done, 1)

                def first(m, par, e):
                    j0 = sum(FTILES[l][:e])
                    for j in range(j0, j0 + FTILES[l][e]):
                        n = n_f1(l) + FTOT[l] * m + j
                        wait(pe, gelu_done, n - 1)
                        rows = 64 if l != 1 and j == 4 else 128
                        w0 = 128 * j
                        split_product(PS[(par * FTOT[l] + j) % 2][0:rows, :], slice(w0, w0 + rows), None, par, 0, 512)\
                            .then_inc(f1_done, 1)

                def router(m, par):
                    for s in range(MT):
                        last = split_product(PS[2][:, s * NE:(s + 1) * NE], slice(NE * FF, WM[1]), None, par,
                                             s * 128, 128, weights_moving=True)
                    last.then_inc(g_ps, 1)

                def second(m, par, e):
                    t0 = (9 * e) // 2
                    pe.wait_ge(gelu_done, n_f1(l) + FTOT[l] * m + min(t0 + FT, FTOT[l]))
                    for s in range(MT):
                        n = (n_unit(l) + EXPERTS[l] * m + e) * MT + s
                        wait(pe, acc_done, n - 1)
                        o = PS[6 + s % 2][:, 0:C]
                        for k in range(FT):
                            slot = t0 + k if l == 1 else 5 * par + k
                            rows = 65 if l != 1 and k == FT - 1 else 128
                            last = mm(o, hm[0:rows, slot, s * 128:(s + 1) * 128], w2[0:rows, FT * e + k, :],
                                      start=(k == 0), stop=(l != 1 and k == FT - 1))
                        if l == 1:
                            last = mm(o, ones[0:1, :], b2[0:1, e, :], start=False, stop=True)
                        last.then_inc(f2_done, 1)

                def mlp_step(m, par, more):
                    pe.wait_ge(h_ready, n_h(l, 1) + m + 1)
                    first(m, par, 0)
                    if l == 1:
                        router(m, par)
                    if more:
                        turn_rows(m + 1, 1 - par)
                    for e in range(1, EXPERTS[l]):
                        first(m, par, e)
                        second(m, par, e - 1)
                    second(m, par, EXPERTS[l] - 1)

                turn_rows(0, 0)
                if l == 0:
                    mlp_step(0, 0, True)
                    mlp_step(1, 1, True)
                with pe.Fori(int(l == 0), NM // 2 - 1) as i:
                    mlp_step(2 * i, 0, True)
                    mlp_step(2 * i + 1, 1, True)
                mlp_step(NM - 2, 0, True)
                mlp_step(NM - 1, 1, False)
            pe.wait_ge(res_done, n_batch(LAYERS, 0))
            pe.wait_ge(ld_skew, 32)
            for c in range(8):
                mm(PS[c][0:NB, :], sc0[:, :], SW0[:, c * 512:(c + 1) * 512], start=True, stop=False)
                mm(PS[c][0:NB, :], sc1[:, :], SW1[:, c * 512:(c + 1) * 512], start=False, stop=True).then_inc(sk_ps, 1)

            def matrices(b0, a, b):
                for s in range(2):
                    rows = slice(s * RD, (s + 1) * RD)
                    for n in range(NHALF):
                        at = (n % 8) * RD
                        last = mm(PS[b0 + 2 * s + n // 8][rows, at:at + RD], a[rows, n, :], b[rows, n, :], start=True, stop=True)
                last.then_inc(r_ps, 1)

            A, A2, A3, A4, BE, BO = M[1], M[2], M[3], M[4], M[5], M[0]
            pe.wait_ge(sk_ev0, 4)
            pe.wait_ge(sk_ev1, 4)
            pe.wait_ge(r_ev, 1)
            matrices(0, A, A)
            pe.wait_ge(r_ev, 5)
            matrices(4, A, A2)
            matrices(0, A2, A2)
            pe.wait_ge(r_ev, 15)
            matrices(0, A4, BE)
            pe.wait_ge(r_ev, 17)
            matrices(4, A4, BO)
            pe.wait_ge(r_ev, 30)
            for q in range(SQUARINGS):
                F, F_T = (FM[0:2] if q % 2 == 0 else FM[2:4])
                if q:
                    pe.wait_ge(r_ev, 30 + 8 * q)
                matrices(0, F_T, F)
                if q + 1 < SQUARINGS:
                    matrices(4, F, F_T)
            F = FM[0] if SQUARINGS % 2 == 0 else FM[2]
            pe.wait_ge(u_dup, 1)
            pe.wait_ge(r_ev, 30 + 8 * SQUARINGS - 4)
            nc.tensor.transpose(PS[7][:, 0:C0], UD[:, 0, :], ident)
            nc.tensor.transpose(PS[7][:, C0:C], UD[0:C - C0, 1, :], ident[0:C - C0, 0:C - C0]).then_inc(u_ps, 1)

            def x_turn(q):
                wait(pe, t_ev, q - 1)
                for s in range(MT):
                    b = MT * q + s
                    nc.tensor.transpose(PS[2 * (q % 2)][:, s * 128:(s + 1) * 128], X[:, b * C:b * C + C0], ident)
                    last = nc.tensor.transpose(PS[2 * (q % 2) + 1][0:C - C0, s * 128:(s + 1) * 128],
                                               X[:, b * C + C0:(b + 1) * C], ident)
                last.then_inc(t_ps, 1)

            def z_product(q):
                rows, at = slice((q // 4) * RD, (q // 4 + 1) * RD), (q % 2) * 512
                pe.wait_ge(t_ev, q + 1)
                wait(pe, z_ev, q)
                mm(PS[4][rows, :], QU[:, 0, :], xT0[:, at:at + 512], start=True, stop=False)
                mm(PS[4][rows, :], QU[0:C - C0, 1, :], xT1[:, at:at + 512], start=False, stop=True).then_inc(z_ps, 1)

            def zr_product(q):
                rows, at = slice((q // 4) * RD, (q // 4 + 1) * RD), (q % 2) * 512
                pe.wait_ge(z_ev, q + 1)
                wait(pe, yy_ev, q)
                for s in range(MT):
                    last = mm(PS[5][rows, s * 128:(s + 1) * 128], F[rows, (MT * q + s) % NHALF, :],
                              zs[rows, at + s * 128:at + (s + 1) * 128], start=True, stop=True)
                last.then_inc(yy_ps, 1)

            def back(q):
                rows, at = slice((q // 4) * RD, (q // 4 + 1) * RD), (q % 2) * 512
                pe.wait_ge(yy_ev, q + 1)
                for h in range(2):
                    wait(pe, o_ev, 2 * q + h - 1)
                    for s in (2 * h, 2 * h + 1):
                        last = mm(PS[6 + h][:, (s % 2) * C:(s % 2 + 1) * C], ys[rows, at + s * 128:at + (s + 1) * 128],
                                  UT[rows, :], start=True, stop=True)
                    last.then_inc(o_ps, 1)

            pe.wait_ge(u_ev, 1)
            x_turn(0)
            for q in range(NM):
                z_product(q)
                if q + 1 < NM:
                    x_turn(q + 1)
                zr_product(q)
                if q:
                    back(q - 1)
            back(NM - 1)

        @block.gpsimd
        def _(pool):
            R = nc.gpsimd
            pool.dma_start(QA[:, 0, :], d["P"][0:C0, :]).then_inc(q_ld, 16)
            R.memset(QA[:, 1, :], 0.0)
            R.memset(QU[:, 1, :], 0.0)
            R.memset(qk_[:, :], 0.0)
            R.memset(qc[:, 0:1], 0.5)
            R.memset(qc[:, 1:2], -1.0).then_inc(q_step, 1)
            pool.wait_ge(q_step, 1)
            pool.dma_start(QA[0:C - C0, 1, :], d["P"][C0:C, :]).then_inc(q_ld, 16)
            pool.wait_ge(ld_cond, 80)
            R.tensor_copy(QU[:, 0, :], K[:, K_EYE:K_EYE + RD]).then_inc(q_step, 1)
            pool.wait_ge(q_step, 2)
            pool.sem_clear(q_step)
            pool.wait_ge(q_ld, 32)
            iota = K[:, K_IOTA:K_IOTA + 1]

            def rows(a):
                return a.rearrange("p (o j) -> p o j", o=1).broadcast_to([128, 2, RD])

            def link(ins, value):
                ins.then_inc(q_step, 1)
                pool.wait_ge(q_step, value)

            with pool.Fori(0, RD) as k:
                ak, vk = QA[:, :, bass.ds(k, 1)], QV[:, :, bass.ds(k, 1)]
                R.tensor_scalar(qs[:, 0:1], iota, qk_[:, 0:1], None, ALU.is_ge)
                link(R.tensor_scalar(qs[:, 1:2], iota, qk_[:, 0:1], None, ALU.is_equal), 1)
                R.tensor_tensor(QV[:, 0, bass.ds(k, 1)], QA[:, 0, bass.ds(k, 1)], qs[:, 0:1], ALU.mult)
                R.tensor_copy(QV[:, 1, bass.ds(k, 1)], QA[:, 1, bass.ds(k, 1)])
                link(R.tensor_scalar(qprod[:, RD:2 * RD], QA[:, 0, :], qs[:, 1:2], None, ALU.mult), 2)
                link(R.tensor_tensor(qtmp[:, :, :], QA[:, :, :], vk.broadcast_to([128, 2, RD]), ALU.mult), 3)
                link(R.tensor_tensor(qprod[:, 0:RD], qtmp[:, 0, :], qtmp[:, 1, :], ALU.add), 4)
                link(R.partition_all_reduce(qsum[:, :], qprod[:, :], 128, RADD), 5)
                sq, al = qsum[:, bass.ds(k, 1)], qsum[:, bass.ds(k + RD, 1)]
                R.tensor_tensor(qs[:, 2:3], sq, qc[:, 0:1], ALU.pow)
                link(R.tensor_copy(qs[:, 3:4], al), 6)
                link(R.tensor_scalar(qs[:, 3:4], qs[:, 3:4], 0.0, 2.0, ALU.is_ge, ALU.mult), 7)
                link(R.tensor_scalar(qs[:, 4:5], qs[:, 3:4], -1.0, qs[:, 2:3], ALU.add, ALU.mult), 8)
                R.tensor_scalar(qs[:, 7:8], qs[:, 1:2], qs[:, 4:5], None, ALU.mult)
                R.tensor_scalar(qw[:, :], qsum[:, RD:2 * RD], qs[:, 4:5], None, ALU.mult)
                link(R.tensor_tensor(qs[:, 5:6], qs[:, 4:5], al, ALU.mult), 9)
                R.tensor_tensor(QV[:, 0, bass.ds(k, 1)], QV[:, 0, bass.ds(k, 1)], qs[:, 7:8], ALU.add)
                R.tensor_tensor(qw[:, :], qw[:, :], qsum[:, 0:RD], ALU.add)
                link(R.tensor_tensor(qs[:, 5:6], qs[:, 5:6], sq, ALU.add), 10)
                link(R.tensor_scalar(qs[:, 6:7], qs[:, 5:6], 1e-37, None, ALU.max), 11)
                link(R.tensor_tensor(qtau[:, bass.ds(k, 1)], qs[:, 6:7], qc[:, 1:2], ALU.pow), 12)
                link(R.tensor_tensor(qw[:, :], qw[:, :], qtau[:, bass.ds(k, 1)].broadcast_to([128, RD]), ALU.mult), 13)
                link(R.tensor_tensor(qtmp[:, :, :], vk.broadcast_to([128, 2, RD]), rows(qw[:, :]), ALU.mult), 14)
                R.tensor_scalar(qk_[:, :], qk_[:, :], 1.0, None, ALU.add)
                link(R.tensor_tensor(QA[:, :, :], QA[:, :, :], qtmp[:, :, :], ALU.subtract), FWD)
                pool.sem_clear(q_step)
            with pool.Fori(0, RD) as k:
                j = RD - 1 - k
                vj = QV[:, :, bass.ds(j, 1)].broadcast_to([128, 2, RD])
                link(R.tensor_tensor(qtmp[:, :, :], QU[:, :, :], vj, ALU.mult), 1)
                link(R.tensor_tensor(qprod[:, 0:RD], qtmp[:, 0, :], qtmp[:, 1, :], ALU.add), 2)
                link(R.partition_all_reduce(qsum[:, 0:RD], qprod[:, 0:RD], 128, RADD), 3)
                link(R.tensor_tensor(qw[:, :], qsum[:, 0:RD], qtau[:, bass.ds(j, 1)].broadcast_to([128, RD]), ALU.mult), 4)
                link(R.tensor_tensor(qtmp[:, :, :], vj, rows(qw[:, :]), ALU.mult), 5)
                link(R.tensor_tensor(QU[:, :, :], QU[:, :, :], qtmp[:, :, :], ALU.subtract), BWD)
                pool.sem_clear(q_step)
            R.memset(qk_[:, :], 0.0).then_inc(qr_done, 1)


def _pad_heads(w, b, row_one):
    wb = np.concatenate([w, b[None]], 0).reshape(C + 1, G, HG, HD)
    o = np.zeros((C + 1, G, HG, HP), np.float32)
    for k in range(3):
        o[:, :, :, k * HD:(k + 1) * HD] = wb
    if row_one:
        o[C, :, :, 3 * HD] = 1.0
    return o.reshape(C + 1, G * 128)


def _constants():
    k = np.zeros((128, K_N), np.float32)
    k[:, K_ID:K_ID + 128] = np.eye(128)
    p = np.arange(128)
    k[:, K_MQ] = -((p % HP >= 2 * HD) & (p % HP < 3 * HD)).astype(np.float32)
    k[:, K_MK] = -((p % HP >= HD) & (p % HP < 2 * HD)).astype(np.float32)
    k[:, K_MH] = -((p >= 2 * C1) & (p < S3)).astype(np.float32)
    k[:, K_MW] = -((p >= C1) & (p < 2 * C1)).astype(np.float32)
    k[:, K_IOTA] = p
    k[:RD, K_EYE:K_EYE + RD] = np.eye(RD)
    j = np.arange(RD)
    k[:, K_SGN:K_SGN + RD] = np.sign(j[None] - (p % RD)[:, None])
    k[:, K_LOW:] = (j[None, :NE] < j[:NE, None]).reshape(-1)
    return k


def _layout(a):
    z = np.zeros
    r = {"x": a["x"], "cond_t": a["cond_1152"].T, "consts": _constants()}
    ada = [(a["L0_cond_W_ada"], a["L0_cond_b_ada"]), (a["L1_cond_w_adaln"], a["L1_cond_b_adaln"]),
           (a["L2_cond_ada_w"], a["L2_cond_ada_b"])]
    gates, cols = [], []
    for w, b in ada:
        wb = np.concatenate([w, b[None]], 0).reshape(C + 1, 6, C)
        gates += [wb[:, 2], wb[:, 5]]
        for kind in (0, 1, 3, 4):
            t = z((C + 1, 3, C1), np.float32)
            t[:, :, :C - C0] = wb[:, kind, None, C0:]
            cols += [wb[:, kind, :C0], t.reshape(C + 1, S3)]
    r["ada_gate"] = np.concatenate(gates, 1)
    r["ada_col"] = np.concatenate(cols, 1)
    lc = z((XW, 4), np.float32)
    for n, name in enumerate(("ln1_w", "ln1_b", "ln2_w", "ln2_b")):
        v = a["L2_cond_" + name]
        t = np.full((3, C1), 1.0 - n % 2, np.float32)
        t[:, :C - C0] = v[C0:]
        lc[:, n] = np.concatenate([v[:C0], t.reshape(-1)])
    r["ln_col"] = lc
    zero = z((C,), np.float32)

    def split3(w, b):
        return [w[:, k * C:(k + 1) * C] for k in range(3)], [b[k * C:(k + 1) * C] for k in range(3)]

    qkv = [split3(a["L0_cond_W_qkv"], a["L0_cond_b_qkv"]), split3(a["L1_cond_w_qkv"], a["L1_cond_b_qkv"]),
           ([a["L2_cond_wq"], a["L2_cond_wk"], a["L2_cond_wv"]], [zero] * 3)]
    for l, (w, b) in enumerate(qkv):
        r[f"wqkv{l}"] = np.concatenate([_pad_heads(w[0], b[0], False), _pad_heads(w[1], b[1], True),
                                        np.concatenate([w[2], b[2][None]], 0)], 1)
    for l, (w, b) in enumerate(((a["L0_cond_W_proj"], a["L0_cond_b_proj"]), (a["L1_cond_w_proj"], a["L1_cond_b_proj"]),
                                (a["L2_cond_wo"], a["L2_cond_wo_b"]))):
        r[f"wp{l}"] = np.concatenate([w, b[None]], 0)
    for l, w1, b1, w2, b2 in ((0, "W_fc1", "b_fc1", "W_fc2", "b_fc2"), (2, "fc1_w", "fc1_b", "fc2_w", "fc2_b")):
        w1, b1, w2, b2 = (a[f"L{l}_cond_{n}"] for n in (w1, b1, w2, b2))
        r[f"wm{l}"] = np.concatenate([w1, b1[None]], 0)
        t = z((FT * 128, C), np.float32)
        t[:FF] = w2
        t[FF] = b2
        r[f"w2_{l}"] = t
    w1 = np.concatenate([a["L1_cond_w1"], a["L1_cond_b1"][:, None]], 1)
    wg = np.concatenate([a["L1_cond_w_gate"], z((1, NE), np.float32)], 0)
    r["wm1"] = np.concatenate([w1.transpose(1, 0, 2).reshape(C + 1, NE * FF), wg], 1)
    t = z((NE, FT * 128, C), np.float32)
    for e in range(NE):
        at = (e % 2) * 64
        t[e, at:at + FF] = a["L1_cond_w2"][e]
    r["w2_1"] = t.reshape(NE * FT * 128, C)
    r["b2_1"] = a["L1_cond_b2"][None]
    iu, ju = np.triu_indices(RD, k=1)
    wb = np.concatenate([a["L3_cond_W"].T, a["L3_cond_b"][None]], 0)
    t = z((C + 1, RD, RD), np.float32)
    t[:, iu, ju] = wb
    t[:, ju, iu] = wb
    r["skew_w"] = t.reshape(C + 1, RD * RD)
    r["P"] = a["L3_cond_P"]
    return {k: np.ascontiguousarray(v) for k, v in r.items()}


def kernel(**inputs):
    import concourse.bacc as _bacc
    from concourse.bass_utils import run_bass_kernel_spmd as _run

    nc = _bacc.Bacc("TRN2", target_bir_lowering=False, num_devices=1)
    arrays, d = {}, {}
    for name, a in _layout({k: np.asarray(v) for k, v in inputs.items()}).items():
        arrays[f"in_{name}"] = a
        d[name] = nc.dram_tensor(f"in_{name}", a.shape, mybir.dt.from_np(a.dtype), kind="ExternalInput").ap()
    out = nc.dram_tensor("out_0", (NB, T, C), F32, kind="ExternalOutput").ap()
    gates_dram = nc.dram_tensor("gates", (NB, GC), F32, kind="Internal").ap()
    skew_dram = nc.dram_tensor("skew", (NB, RD * RD), F32, kind="Internal").ap()
    program(nc, d, out, gates_dram, skew_dram)
    r = _run(nc, [arrays], core_ids=[0])
    return r.results[0]["out_0"]
```

```python
import numpy as np
import concourse.bass as bass
from concourse import mybir
from contextlib import ExitStack

F32 = mybir.dt.float32
F32R = mybir.dt.float32r
ALU = mybir.AluOpType
ACT = mybir.ActivationFunctionType
AX = mybir.AxisListType

NB, T, C = 32, 128, 144
NH, HD = 16, 9
LAYERS = 3
C0 = 128
C1 = C - C0 + 1
S3 = 3 * C1
XW = C0 + S3
G, HG, HP = 4, 4, 32
WQKV = 2 * G * 128 + C
FF = 4 * C
NE = 4
EXPERTS = (1, NE, 1)
FTILES = ((5,), (5, 4, 5, 4), (5,))
FTOT = tuple(sum(f) for f in FTILES)
WM = (FF, NE * FF + NE, FF)
WMX = max(WM)
FT = 5
MT = 4
NM = NB // MT
RD = 64
SQUARINGS = 6
EPS = (1e-6, 1e-6, 1e-5)
GC = LAYERS * 2 * C
SPLIT_PIECES = (WMX + 511) // 512
SPLITS = 2 + 2 * SPLIT_PIECES
NHALF = NB // 2
K_ID, K_MQ, K_MK, K_MH, K_MW, K_IOTA, K_EYE, K_SGN, K_LOW = 0, 128, 129, 130, 131, 132, 133, 197, 261
K_N = K_LOW + NE * NE
FWD, BWD = 15, 6
RADD = bass.bass_isa.ReduceOp.add


def wait(eng, sem, value):
    if isinstance(value, int) and value <= 0:
        return
    eng.wait_ge(sem, value)


def cut(start, size):
    return slice(start, start + size) if isinstance(start, int) else bass.ds(start, size)


def program(nc, d, out, gates_dram, skew_dram):
    ctx = ExitStack()
    with ctx:
        def sb(name, shape, dt=F32):
            return ctx.enter_context(nc.sbuf_tensor(name, shape, dt))

        def sem(name):
            return ctx.enter_context(nc.semaphore(name))

        X = sb("X", [128, NB * C])
        K = sb("K", [128, K_N])
        ident = K[:, K_ID:K_ID + 128]
        st6 = sb("st6", [128, NB, 6])
        mean = sb("mean", [128, NB])
        var = sb("var", [128, NB])
        rstd = sb("rstd", [128, NB])
        rtmp = sb("rtmp", [128, 3, NB])
        epst = sb("epst", [128, 3])
        sc0, sc1 = sb("sc0", [C0, NB]), sb("sc1", [C1, NB])
        ctmp = sb("ctmp", [128, 4, NB])
        col0 = sb("col0", [C0, LAYERS, 4, NB])
        col1 = sb("col1", [S3, LAYERS, 4, NB])
        lnc = sb("lnc", [128, 8])
        Whi, Wlo = sb("Whi", [C0, WMX], F32R), sb("Wlo", [C0, WMX], F32R)
        W3 = sb("W3", [S3, WMX], F32R)
        wp0, wp1 = sb("wp0", [C0, 2, C]), sb("wp1", [C1, 2, C])
        w2 = sb("w2", [128, NE * FT, C])
        b2 = sb("b2", [1, NE, C])
        ones = sb("ones", [1, 128])
        xh = sb("xh", [128, 2 * MT, XW])
        hf = sb("hf", [128, MT * 128])
        hs = sb("hs", [S3, MT * 128])
        hshi = sb("hshi", [S3, MT * 128], F32R)
        hhi, hlo = sb("hhi", [128, 2, MT * 128], F32R), sb("hlo", [128, 2, MT * 128], F32R)
        h3 = sb("h3", [S3, 2, MT * 128], F32R)
        Q = sb("Q", [128, 2, G, 256], F32R)
        kst = sb("kst", [128, 512], F32R)
        KBD = sb("KBD", [128, 2, G, HG, 256], F32R)
        qkhi = sb("qkhi", [128, 512], F32R)
        gate = sb("gate", [128, 4, C])
        ytmp = sb("ytmp", [128, C])
        BIG = sb("BIG", [128, 10240 + 2 * WMX])
        VA = BIG[:, 0:2048].rearrange("p (b h w) -> p b h w", b=4, h=NH)
        PT = BIG[:, 2048:6144].rearrange("p (b r n) -> p b r n", b=2, r=HG)
        OTs = BIG[:, 6144:7168].rearrange("p (b n) -> p b n", b=2)
        oq = BIG[:, 7168:7168 + 2 * (C + 1)].rearrange("p (b n) -> p b n", b=2)
        oT = BIG[:, 7500:8012].rearrange("p (b n) -> p b n", b=2)
        rsum = BIG[:, 8012:8044].rearrange("p (b n) -> p b n", b=2)
        nmax = BIG[:, 8192:8704].rearrange("p (g n) -> p g n", g=G)
        hm = BIG[:, 0:9216].rearrange("p (t n) -> p t n", n=512)
        acc = BIG[:, 9216:9792]
        rt = BIG[:, 9792:10240]
        RAW0 = 10240
        WR = BIG[:, RAW0:RAW0 + WMX]
        WR3 = BIG[0:S3, RAW0 + WMX:RAW0 + 2 * WMX]
        gate_rows = BIG[0:NB, 9000:9000 + GC]
        mgate = sb("mgate", [128, 2, MT * C])

        QA, QV, QU = (sb(n, [128, 2, RD]) for n in ("QA", "QV", "QU"))
        qprod, qsum, qtmp, qw, qtau = (sb("qprod", [128, 2 * RD]), sb("qsum", [128, 2 * RD]), sb("qtmp", [128, 2, RD]),
                                       sb("qw", [128, RD]), sb("qtau", [128, RD]))
        qk_, qs, qc = sb("qcount", [128, 1]), sb("qscalars", [128, 8]), sb("qexponents", [128, 2])
        UD = BIG[:, 12288:12288 + 4 * RD].rearrange("p (k j) -> p k j", k=2)
        UT = BIG[:, 12544:12544 + C]
        SW0, SW1 = BIG[:, RAW0:RAW0 + RD * RD], BIG[0:C1, RD * RD:2 * RD * RD]
        SV = BIG[0:NB, 0:RD * RD]
        M = [BIG[:, RD * RD + k * NHALF * RD:RD * RD + (k + 1) * NHALF * RD].rearrange("p (n j) -> p n j", n=NHALF)
             for k in range(8)]
        FM = M[1:5]
        xT0, xT1 = BIG[:, 0:1024], BIG[0:C - C0, 1024:2048]
        zs, ys = BIG[:, 2048:3072], BIG[:, 3072:4096]

        PS = [ctx.enter_context(nc.psum_tensor(f"PS{n}", [128, 512], F32)) for n in range(8)]

        ld_cond, ld_ada, ld_gw, ld_x, ld_skew = (sem("cond_loaded"), sem("ada_loaded"), sem("gate_weights_loaded"),
                                                       sem("x_loaded"), sem("skew_loaded"))
        ld_wq, ld_wm, ld_wp, ld_w2 = sem("wqkv_loaded"), sem("wm_loaded"), sem("wp_loaded"), sem("w2_loaded")
        s_split = sem("weights_split")
        s_e, s_silu, s_const = sem("cond_exp"), sem("silu_steps"), sem("constants_set")
        s_gps, s_gev, s_gst, s_cps, s_cev = (sem("gates_product"), sem("gates_copied"), sem("gates_stored"),
                                             sem("columns_product"), sem("columns_ready"))
        s_cln = sem("columns_steps")
        s_st0, s_var, s_std, s_ln = sem("first_stats"), sem("variance_ready"), sem("std_ready"), sem("rstd_steps")
        xh_ready, xt_done = sem("xh_ready"), sem("xt_done")
        hf_ready, hhi_ready, h_ready = sem("hf_ready"), sem("hhi_ready"), sem("h_ready")
        qk_ps, qk_hi, qk_lo = sem("qk_product"), sem("qk_high"), sem("qk_stacked")
        v_ps, v_ev, va_set = sem("v_product"), sem("v_ready"), sem("va_set")
        s1_done, max_done = sem("s1_done"), sem("max_done")
        mt_done, mrow = sem("max_transposed"), sem("max_row_written")
        s2_done, exp_done = sem("s2_done"), sem("exp_done")
        pv_done, ot_ev = sem("pv_done"), sem("ot_copied")
        otr_done, rs_done, norm_done = sem("o_back"), sem("rsum_done"), sem("o_normalised")
        ot2_done, oT_ev = sem("o_transposed"), sem("oT_copied")
        y_done, y_read, x_new, res_done = (sem("proj_done"), sem("y_gated"), sem("x_updated"),
                                            sem("res_done"))
        gate_ld = [sem(f"gate_loaded{n}") for n in range(4)]
        kbd_a, kbd_v = sem("kbd_by_act"), sem("kbd_by_dve")
        f1_done, gelu_done = sem("fc1_done"), sem("gelu_done")
        f2_done, acc_done = sem("fc2_done"), sem("expert_added")
        hm_ones = sem("hm_ones_set")
        g_ps, g_steps, g_th = sem("router_product"), sem("router_steps"), sem("router_tanh")
        m_gate = [sem("mlp_gate_loaded0"), sem("mlp_gate_loaded1")]

        q_ld, q_step, qr_done = sem("p_loaded"), sem("qr_step"), sem("u_ready")
        sk_ps, sk_ev0, sk_ev1, sk_st, sk_ld = (sem("skew_product"), sem("skew_copied_by_dve"), sem("skew_copied_by_act"),
                                       sem("skew_stored"), sem("skew_back"))
        r_ps, r_ev = sem("matrix_product"), sem("matrix_step")
        u_dup, u_ps, u_ev = sem("u_doubled"), sem("u_turned"), sem("ut_ready")
        t_ps, t_ev, z_ps, z_ev, yy_ps, yy_ev, o_ps, o_ev, s_out = (
            sem("x_turned"), sem("xT_copied"), sem("z_product"), sem("z_copied"), sem("zr_product"), sem("zr_copied"),
            sem("rotated"), sem("x_rotated"), sem("output_stored"))

        def n_batch(l, mlp):
            return (2 * l + mlp) * NB

        def n_gated(l, mlp):
            return (l + mlp + int(l == 2)) * NB

        def n_h(l, mlp):
            return l * (NB // 2 + NM) + mlp * (NB // 2)

        def n_unit(l):
            return sum(EXPERTS[:l]) * NM

        def n_f1(l):
            return sum(FTOT[:l]) * NM

        def xb(b, lo=0, hi=C):
            return X[:, cut(b * C + lo, hi - lo)]

        block = ctx.enter_context(nc.Block())

        @block.sync
        def _(sp):
            sp.dma_start(ctmp[:, 0, :], d["cond_t"][0:C0, :]).then_inc(ld_cond, 16)
            sp.dma_start(ctmp[0:C - C0, 1, :], d["cond_t"][C0:C, :]).then_inc(ld_cond, 16)
            sp.dma_start(K[:, :], d["consts"]).then_inc(ld_cond, 16)
            sp.dma_start(lnc[:, 0:4], d["ln_col"][0:C0, :]).then_inc(ld_cond, 16)
            sp.dma_start(lnc[0:S3, 4:8], d["ln_col"][C0:XW, :]).then_inc(ld_cond, 16)
            sp.dma_start(BIG[:, 0:GC], d["ada_gate"][0:C0, :]).then_inc(ld_gw, 16)
            sp.dma_start(BIG[0:C1, GC:2 * GC], d["ada_gate"][C0:C + 1, :]).then_inc(ld_gw, 16)
            for q in range(4):
                sp.dma_start(X[:, q * 8 * C:(q + 1) * 8 * C].rearrange("p (b c) -> p b c", b=8),
                             d["x"][q * 8:(q + 1) * 8].rearrange("b t c -> t b c")).then_inc(ld_x, 16)
            A0 = 2 * GC
            sp.dma_start(BIG[:, A0:A0 + LAYERS * 4 * XW], d["ada_col"][0:C0, :]).then_inc(ld_ada, 16)
            sp.dma_start(BIG[0:C1, A0 + LAYERS * 4 * XW:A0 + 2 * LAYERS * 4 * XW], d["ada_col"][C0:C + 1, :]).then_inc(ld_ada, 16)

            def load_raw(name, n, s):
                sp.dma_start(WR[:, 0:n], d[name][0:C0, :]).then_inc(s, 16)
                for k in range(3):
                    sp.dma_start(WR3[k * C1:(k + 1) * C1, 0:n], d[name][C0:C + 1, :]).then_inc(s, 16)

            def load_wp(l):
                sp.dma_start(wp0[:, l % 2, :], d[f"wp{l}"][0:C0, :]).then_inc(ld_wp, 16)
                sp.dma_start(wp1[:, l % 2, :], d[f"wp{l}"][C0:C + 1, :]).then_inc(ld_wp, 16)

            load_raw("wqkv0", WQKV, ld_wq)
            load_wp(0)
            sp.wait_ge(s_gev, 2)
            sp.dma_start(gates_dram, gate_rows).then_inc(s_gst, 16)
            sp.wait_ge(s_gst, 16)
            for l in range(LAYERS):
                sp.wait_ge(s_split, SPLITS * (2 * l + 1))
                load_raw(f"wm{l}", WM[l], ld_wm)
                wait(sp, f2_done, n_unit(l) * MT)
                nt = EXPERTS[l] * FT
                sp.dma_start(w2[:, 0:nt, :], d[f"w2_{l}"].rearrange("(t p) c -> p t c", p=128)).then_inc(ld_w2, 16)
                if l == 1:
                    sp.dma_start(b2[:, :, :], d["b2_1"]).then_inc(ld_w2, 16)

                def sp_step(b, u):
                    wait(sp, res_done, n_batch(l, 0) + b - 3)
                    sp.dma_start(gate[:, u, :], gates_dram[cut(b, 1), 2 * l * C:(2 * l + 1) * C]
                                 .broadcast_to([128, C])).then_inc(gate_ld[u], 16)

                for b in range(4):
                    sp_step(b, b)
                with sp.Fori(1, NB // 4) as i:
                    for u in range(4):
                        sp_step(4 * i + u, u)

                sp.wait_ge(s_split, SPLITS * (2 * l + 2))
                if l + 1 == LAYERS:
                    sp.dma_start(SW0, d["skew_w"][0:C0, :]).then_inc(ld_skew, 16)
                else:
                    load_raw(f"wqkv{l + 1}", WQKV, ld_wq)
                    load_wp(l + 1)

                def load_mlp_gate(m, par):
                    wait(sp, res_done, n_batch(l, 1) + MT * (m - 1))
                    for s in range(MT):
                        sp.dma_start(mgate[:, par, s * C:(s + 1) * C],
                                     gates_dram[cut(MT * m + s, 1), (2 * l + 1) * C:(2 * l + 2) * C]
                                     .broadcast_to([128, C])).then_inc(m_gate[par], 16)

                load_mlp_gate(0, 0)
                load_mlp_gate(1, 1)
                with sp.Fori(1, NM // 2) as i:
                    load_mlp_gate(2 * i, 0)
                    load_mlp_gate(2 * i + 1, 1)
            sp.wait_ge(res_done, n_batch(LAYERS, 0))
            sp.dma_start(SW1, d["skew_w"][C0:C + 1, :]).then_inc(ld_skew, 16)
            sp.wait_ge(sk_ev0, 4)
            sp.wait_ge(sk_ev1, 4)
            sp.dma_start(skew_dram, SV).then_inc(sk_st, 16)
            sp.wait_ge(sk_st, 16)
            for s in range(2):
                sp.dma_start(M[0][s * RD:(s + 1) * RD, :, :],
                             skew_dram[s * NHALF:(s + 1) * NHALF, :].rearrange("n (i j) -> i n j", i=RD)).then_inc(sk_ld, 16)
            for q in range(NM):
                sp.wait_ge(o_ev, 2 * q + 2)
                sp.dma_start(out[MT * q:MT * (q + 1)].rearrange("b t c -> t b c"),
                             X[:, MT * q * C:MT * (q + 1) * C].rearrange("p (b c) -> p b c", b=MT)).then_inc(s_out, 16)
            sp.wait_ge(s_out, 16 * NM)

        @block.vector
        def _(dve):
            V = nc.vector
            V.memset(sc1[:, :], 1.0).then_inc(s_silu, 1)
            V.memset(ones[:, :], 1.0)
            V.memset(KBD[:, :, :, :, :].bitcast(F32), 0.0)
            V.memset(xh[:, :, :], 1.0)
            V.memset(epst[:, 0:1], EPS[0])
            V.memset(epst[:, 1:2], EPS[2]).then_inc(s_const, 1)
            dve.wait_ge(s_e, 2)
            V.tensor_scalar(ctmp[:, 2, :], ctmp[:, 2, :], 1.0, None, ALU.add)
            V.tensor_scalar(ctmp[0:C - C0, 3, :], ctmp[0:C - C0, 3, :], 1.0, None, ALU.add).then_inc(s_silu, 1)
            dve.wait_ge(s_silu, 2)
            V.reciprocal(ctmp[:, 2, :], ctmp[:, 2, :])
            V.reciprocal(ctmp[0:C - C0, 3, :], ctmp[0:C - C0, 3, :]).then_inc(s_silu, 1)
            dve.wait_ge(s_silu, 3)
            V.tensor_tensor(sc0[:, :], ctmp[:, 0, :], ctmp[:, 2, :], ALU.mult)
            V.tensor_tensor(sc1[0:C - C0, :], ctmp[0:C - C0, 1, :], ctmp[0:C - C0, 3, :], ALU.mult).then_inc(s_silu, 1)
            dve.wait_ge(ld_x, 64)

            with dve.Fori(0, NB) as b:
                V.bn_stats(st6[:, cut(b, 1), :], xb(b)).then_inc(s_st0, 1)
            for n in range(2):
                dve.wait_ge(s_gps, n + 1)
                V.tensor_copy(gate_rows[:, n * GC // 2:(n + 1) * GC // 2], PS[n][0:NB, 0:GC // 2]).then_inc(s_gev, 1)
            for l in range(LAYERS):
                dve.wait_ge(s_cps, l + 1)
                for kind in range(4):
                    for t, ps, rows in ((col0, PS[2 + 2 * (l % 2)], C0), (col1, PS[3 + 2 * (l % 2)], S3)):
                        one = float(kind % 2)
                        last = V.tensor_scalar(t[0:rows, l, kind, :], ps[0:rows, kind * NB:(kind + 1) * NB], one, None, ALU.add)
                last.then_inc(s_cev, 1)
            dve.wait_ge(s_cev, LAYERS)
            L2 = LAYERS - 1
            for ph in range(2):
                for t, rows, c in ((col0, C0, 0), (col1, S3, 4)):
                    w_, b_ = lnc[0:rows, c + 2 * ph:c + 2 * ph + 1], lnc[0:rows, c + 2 * ph + 1:c + 2 * ph + 2]
                    last = V.scalar_tensor_tensor(t[0:rows, L2, 2 * ph, :], t[0:rows, L2, 2 * ph + 1, :], b_,
                                                  t[0:rows, L2, 2 * ph, :], ALU.mult, ALU.add)
            last.then_inc(s_cln, 1)
            dve.wait_ge(s_cln, 1)
            for ph in range(2):
                for t, rows, c in ((col0, C0, 0), (col1, S3, 4)):
                    last = V.tensor_scalar(t[0:rows, L2, 2 * ph + 1, :], t[0:rows, L2, 2 * ph + 1, :],
                                           lnc[0:rows, c + 2 * ph:c + 2 * ph + 1], None, ALU.mult)
            last.then_inc(s_cln, 1)
            dve.wait_ge(s_cln, 2)

            def split(n, k):
                V.tensor_copy(Whi[:, 0:n], WR[:, 0:n]).then_inc(s_split, 1)
                dve.wait_ge(s_split, SPLITS * k + 1)
                V.tensor_tensor(Wlo[:, 0:n], WR[:, 0:n], Whi[:, 0:n].bitcast(F32), ALU.subtract).then_inc(s_split, 1)
                for q in range(SPLIT_PIECES):
                    lo, hi = q * 512, min((q + 1) * 512, n)
                    if lo < n:
                        V.tensor_copy(hshi[:, 0:hi - lo], WR3[:, lo:hi]).then_inc(s_split, 1)
                        dve.wait_ge(s_split, SPLITS * k + 3 + 2 * q)
                        V.scalar_tensor_tensor(W3[:, lo:hi], hshi[:, 0:hi - lo].bitcast(F32), K[0:S3, K_MW:K_MW + 1],
                                               WR3[:, lo:hi], ALU.mult, ALU.add).then_inc(s_split, 1)
                        dve.wait_ge(s_split, SPLITS * k + 4 + 2 * q)
                done = 2 + 2 * ((n + 511) // 512)
                if done < SPLITS:
                    V.memset(epst[:, 2:3], 0.0).then_inc(s_split, SPLITS - done)

            def rstd_all(l, mlp):
                ph = 2 * l + mlp
                eps = epst[:, l // 2:l // 2 + 1]
                dve.wait_ge(s_st0, NB) if ph == 0 else dve.wait_ge(res_done, n_batch(l, mlp))
                V.tensor_tensor(mean[:, :], st6[:, :, 1], st6[:, :, 4], ALU.add)
                V.tensor_tensor(rtmp[:, 0, :], st6[:, :, 1], st6[:, :, 4], ALU.subtract)
                V.tensor_tensor(var[:, :], st6[:, :, 2], st6[:, :, 5], ALU.add).then_inc(s_var, 1)
                dve.wait_ge(s_var, 4 * ph + 1)
                V.tensor_scalar(mean[:, :], mean[:, :], 0.5, None, ALU.mult)
                V.tensor_scalar(var[:, :], var[:, :], 1.0 / C, None, ALU.mult)
                V.tensor_tensor(rtmp[:, 0, :], rtmp[:, 0, :], rtmp[:, 0, :], ALU.mult).then_inc(s_var, 1)
                dve.wait_ge(s_var, 4 * ph + 2)
                V.scalar_tensor_tensor(var[:, :], rtmp[:, 0, :], 0.25, var[:, :], ALU.mult, ALU.add).then_inc(s_var, 2)
                dve.wait_ge(s_std, ph + 1)
                V.reciprocal(rtmp[:, 1, :], rtmp[:, 0, :])
                V.tensor_scalar(rtmp[:, 2, :], var[:, :], eps, -0.5, ALU.add, ALU.mult).then_inc(s_ln, 1)
                dve.wait_ge(s_ln, 5 * ph + 1)
                V.tensor_tensor(rtmp[:, 2, :], rtmp[:, 2, :], rtmp[:, 1, :], ALU.mult).then_inc(s_ln, 1)
                dve.wait_ge(s_ln, 5 * ph + 2)
                V.tensor_tensor(rtmp[:, 2, :], rtmp[:, 2, :], rtmp[:, 1, :], ALU.mult).then_inc(s_ln, 1)
                dve.wait_ge(s_ln, 5 * ph + 3)
                V.tensor_scalar(rtmp[:, 2, :], rtmp[:, 2, :], 1.5, None, ALU.add).then_inc(s_ln, 1)
                dve.wait_ge(s_ln, 5 * ph + 4)
                V.tensor_tensor(rstd[:, :], rtmp[:, 2, :], rtmp[:, 1, :], ALU.mult).then_inc(s_ln, 1)
                dve.wait_ge(s_ln, 5 * ph + 5)

            def normalise(b, slot):
                mu, rs = mean[:, cut(b, 1)], rstd[:, cut(b, 1)]
                V.tensor_scalar(xh[:, slot, 0:C0], xb(b, 0, C0), mu, rs, ALU.subtract, ALU.mult)
                tail = xh[:, slot, C0:XW].rearrange("p (k c) -> p k c", k=3)[:, :, 0:C1 - 1]
                src = xb(b, C0, C).rearrange("p (o c) -> p o c", o=1).broadcast_to([128, 3, C1 - 1])
                V.tensor_scalar(tail, src, mu, rs, ALU.subtract, ALU.mult).then_inc(xh_ready, 1)

            def low_parts(par, n):
                V.tensor_tensor(hlo[:, par, 0:n], hf[:, 0:n], hhi[:, par, 0:n].bitcast(F32), ALU.subtract)
                V.scalar_tensor_tensor(h3[:, par, 0:n], hshi[:, 0:n].bitcast(F32), K[0:S3, K_MH:K_MH + 1], hs[:, 0:n],
                                       ALU.mult, ALU.add).then_inc(h_ready, 1)

            def gated(y_ps, g):
                V.tensor_tensor(ytmp[:, :], y_ps, g, ALU.mult).then_inc(y_read, 1)

            def added(ny, n, b):
                dve.wait_ge(y_read, ny + 1)
                V.tensor_tensor(xb(b), xb(b), ytmp[:, :], ALU.add).then_inc(x_new, 1)
                dve.wait_ge(x_new, n + 1)
                dve.wait_ge(s_const, 1)
                V.bn_stats(st6[:, cut(b, 1), :], xb(b)).then_inc(res_done, 1)

            for l in range(LAYERS):
                if l == 0:
                    dve.wait_ge(ld_wq, 64)
                    dve.wait_ge(s_cps, LAYERS)
                    split(WQKV, 0)
                rstd_all(l, 0)
                for b in range(4):
                    normalise(b, b)
                if l:
                    dve.wait_ge(f2_done, n_unit(l) * MT)
                V.memset(nmax[:, :, :], 0.0)
                V.memset(BIG[:, 0:2048], 0.0).then_inc(va_set, 1)
                dve.wait_ge(va_set, 3 * l + 1)
                V.memset(VA[:, :, :, HD:HD + 1], 1.0).then_inc(va_set, 1)
                V.memset(oq[:, :, C:C + 1], 1.0).then_inc(va_set, 1)

                def h_second(P, par):
                    dve.wait_ge(hhi_ready, n_h(l, 0) + P + 1)
                    wait(dve, v_ps, NB // 2 * l + P - 1)
                    low_parts(par, 256)

                def qk_stack(pn, par, j):
                    n = 4 * pn + j
                    dve.wait_ge(qk_hi, n + 1)
                    m = K[:, (K_MK, K_MQ)[j // 2]:(K_MK, K_MQ)[j // 2] + 1]
                    if j >= 2:
                        o = Q[:, par, 2 * j - 4:2 * j - 2, :].rearrange("p g n -> p (g n)")
                    else:
                        o = kst[:, :]
                        wait(dve, kbd_a, 2 * pn + j)
                        wait(dve, kbd_v, 2 * pn + j)
                    V.scalar_tensor_tensor(o, qkhi[:, :].bitcast(F32), m, PS[4][:, :], ALU.mult, ALU.add).then_inc(qk_lo, 1)

                def k_diagonal(pn, par, j):
                    dve.wait_ge(qk_lo, 4 * pn + j + 1)
                    for r in (2, 3):
                        rows = slice(HP * r, HP * (r + 1))
                        last = V.tensor_copy(KBD[rows, par, 2 * j:2 * j + 2, r, :],
                                             kst[rows, :].rearrange("p (g n) -> p g n", g=2))
                    last.then_inc(kbd_v, 1)

                def values(P, par):
                    dve.wait_ge(v_ps, NB // 2 * l + P + 1)
                    for s in range(2):
                        last = V.tensor_copy(VA[:, 2 * par + s, :, 0:HD],
                                             PS[5][:, s * C:(s + 1) * C].rearrange("p (h w) -> p h w", h=NH))
                    last.then_inc(v_ev, 1)

                def row_max(b, u, g):
                    n = 4 * (NB * l + b) + g
                    dve.wait_ge(s1_done, n + 1)
                    V.tensor_reduce(nmax[:, g, 3 * HD::HP], PS[g % 2][:, :].rearrange("p (r k) -> p r k", r=HG),
                                    AX.X, ALU.max, negate=True).then_inc(max_done, 1)

                def max_row(b, u):
                    dve.wait_ge(mt_done, NB * l + b + 1)
                    q = Q[:, u // 2, :, (u % 2) * 128:(u % 2) * 128 + 128]
                    V.tensor_tensor(q, q.bitcast(F32), PS[5][:, :].rearrange("p (g n) -> p g n", g=G), ALU.add).then_inc(mrow, 1)

                def inverse_sums(b, u):
                    dve.wait_ge(otr_done, NB * l + b + 1)
                    V.reciprocal(rsum[:, u % 2, :], PS[7][:, :].rearrange("p (h w) -> p h w", w=HP)[:, :, HD]).then_inc(rs_done, 1)

                def normalise_out(b, u):
                    dve.wait_ge(rs_done, NB * l + b + 1)
                    V.tensor_tensor(oq[:, u % 2, 0:C].rearrange("p (h w) -> p h w", h=NH),
                                    PS[7][:, :].rearrange("p (h w) -> p h w", w=HP)[:, :, 0:HD],
                                    rsum[:, u % 2, :].rearrange("p (h o) -> p h o", o=1).broadcast_to([128, NH, HD]),
                                    ALU.mult).then_inc(norm_done, 1)

                def step(t, u, i=None):
                    static = i is None
                    P, par, odd = (t // 2 if static else 2 * i + u // 2), u // 2, u % 2
                    pn = NB // 2 * l + P + 1
                    live = not static or t < NB
                    nxt = not static or P + 1 < NB // 2
                    nxt2 = not static or P + 2 < NB // 2
                    tail = not static or t >= 2
                    ub = (u + 2) % 4
                    gi = None if static else (i - 1 if u < 2 else i)
                    if live:
                        row_max(t, u, 0)
                    if live and odd and nxt:
                        qk_stack(pn, 1 - par, 1)
                    if live:
                        row_max(t, u, 1)
                    if tail:
                        inverse_sums(t - 2, ub)
                    if live and odd and nxt:
                        k_diagonal(pn, 1 - par, 1)
                    if tail:
                        normalise_out(t - 2, ub)
                    if live:
                        row_max(t, u, 2)
                    if live and not odd and not (static and t == 0):
                        values(P, par)
                    if live and odd and nxt:
                        qk_stack(pn, 1 - par, 2)
                    if live:
                        row_max(t, u, 3)
                    if not odd and (not static or t + 4 < NB):
                        normalise(t + 4, u)
                        normalise(t + 5, u + 1)
                    if live and nxt:
                        qk_stack(pn, 1 - par, 3 if odd else 0)
                    if live:
                        max_row(t, u)
                    if tail:
                        gated_at(t - 2, ub, gi)
                    if live and nxt and not odd:
                        k_diagonal(pn, 1 - par, 0)
                    if live and odd and nxt2:
                        h_second(P + 2, par)
                    if tail:
                        added(n_gated(l, 0) + t - 2, n_batch(l, 0) + t - 2, t - 2)

                def gated_at(b, u, gi):
                    dve.wait_ge(y_done, NB * l + b + 1)
                    dve.wait_ge(gate_ld[u], 16 * (NB // 4 * l + b // 4 + 1) if gi is None else 16 * (gi + NB // 4 * l + 1))
                    gated(PS[7][:, 0:C], gate[:, u, :])

                h_second(0, 0)
                for j in range(4):
                    qk_stack(NB // 2 * l, 0, j)
                    if j < 2:
                        k_diagonal(NB // 2 * l, 0, j)
                values(0, 0)
                h_second(1, 1)
                for t in range(4):
                    step(t, t)
                with dve.Fori(1, NB // 4 - 1) as i:
                    for u in range(4):
                        step(4 * i + u, u, i)
                for t in range(NB - 4, NB):
                    step(t, t % 4)
                dve.wait_ge(ld_wm, 64 * (l + 1))
                dve.wait_ge(v_ps, NB // 2 * (l + 1))
                split(WM[l], 2 * l + 1)
                for t in range(NB, NB + 2):
                    step(t, t % 4)

                dve.wait_ge(res_done, n_batch(l, 1))
                rstd_all(l, 1)
                if l != 1:
                    dve.wait_ge(y_done, NB * (l + 1))
                    V.memset(hm[64:65, 4, :], 1.0)
                    V.memset(hm[64:65, 9, :], 1.0).then_inc(hm_ones, 1)

                def mlp_rows(m, par):
                    for s in range(MT):
                        normalise(MT * m + s, MT * par + s)

                def mlp_low(m, par):
                    dve.wait_ge(hhi_ready, n_h(l, 1) + m + 1)
                    wait(dve, f1_done, n_f1(l) + FTOT[l] * (m - 1))
                    low_parts(par, 512)

                def router(m):
                    n0 = 12 * m
                    lg, gt, eq, rk, r0, r1, t0, t1, m0, m1, df, th, cw = (
                        rt[:, 0:16], rt[:, 16:80], rt[:, 80:144], rt[:, 144:160], rt[:, 160:176], rt[:, 176:192],
                        rt[:, 192:208], rt[:, 208:224], rt[:, 224:228], rt[:, 228:232], rt[:, 232:236], rt[:, 236:240],
                        rt[:, 240:256])

                    def q4(a):
                        return a.rearrange("p (s e j) -> p s e j", s=MT, e=NE)

                    lj = lg.rearrange("p (s o j) -> p s o j", s=MT, o=1).broadcast_to([128, MT, NE, NE])
                    le = lg.rearrange("p (s e o) -> p s e o", s=MT, o=1).broadcast_to([128, MT, NE, NE])
                    low = K[:, K_LOW:K_N].rearrange("p (o e j) -> p o e j", o=1, e=NE).broadcast_to([128, MT, NE, NE])
                    dve.wait_ge(g_ps, m + 1)
                    V.tensor_copy(lg, PS[2][:, 0:16]).then_inc(g_steps, 1)
                    dve.wait_ge(g_steps, n0 + 1)
                    V.tensor_tensor(q4(gt), lj, le, ALU.is_gt)
                    V.tensor_tensor(q4(eq), lj, le, ALU.is_equal).then_inc(g_steps, 1)
                    dve.wait_ge(g_steps, n0 + 2)
                    V.tensor_tensor(q4(eq), q4(eq), low, ALU.mult).then_inc(g_steps, 1)
                    dve.wait_ge(g_steps, n0 + 3)
                    V.tensor_tensor(gt, gt, eq, ALU.add).then_inc(g_steps, 1)
                    dve.wait_ge(g_steps, n0 + 4)
                    V.tensor_reduce(rk, gt.rearrange("p (a j) -> p a j", j=NE), AX.X, ALU.add).then_inc(g_steps, 1)
                    dve.wait_ge(g_steps, n0 + 5)
                    V.tensor_scalar(r0, rk, 0.0, 0.5, ALU.is_equal, ALU.mult)
                    V.tensor_scalar(r1, rk, 1.0, 0.5, ALU.is_equal, ALU.mult).then_inc(g_steps, 1)
                    dve.wait_ge(g_steps, n0 + 6)
                    V.tensor_tensor(t0, r0, lg, ALU.mult)
                    V.tensor_tensor(t1, r1, lg, ALU.mult).then_inc(g_steps, 1)
                    dve.wait_ge(g_steps, n0 + 7)
                    V.tensor_reduce(m0, t0.rearrange("p (s e) -> p s e", s=MT), AX.X, ALU.add)
                    V.tensor_reduce(m1, t1.rearrange("p (s e) -> p s e", s=MT), AX.X, ALU.add).then_inc(g_steps, 1)
                    dve.wait_ge(g_steps, n0 + 8)
                    V.tensor_tensor(df, m0, m1, ALU.subtract).then_inc(g_steps, 1)
                    V.tensor_tensor(t0, r0, r1, ALU.subtract)
                    V.tensor_tensor(t1, r0, r1, ALU.add).then_inc(g_steps, 1)
                    dve.wait_ge(g_th, m + 1)
                    dve.wait_ge(g_steps, n0 + 10)
                    thb = th.rearrange("p (s o) -> p s o", o=1).broadcast_to([128, MT, NE])
                    V.tensor_tensor(t0.rearrange("p (s e) -> p s e", s=MT), t0.rearrange("p (s e) -> p s e", s=MT), thb,
                                    ALU.mult).then_inc(g_steps, 1)
                    dve.wait_ge(g_steps, n0 + 11)
                    V.tensor_tensor(cw, t0, t1, ALU.add).then_inc(g_steps, 1)
                    dve.wait_ge(g_steps, n0 + 12)

                cw = rt[:, 240:256]

                def expert_sums(m, e, batches, split_next, gate_par=None, gr=None):
                    if split_next:
                        dve.wait_ge(ld_wq, 64 * (l + 2))
                        dve.wait_ge(f1_done, n_f1(l + 1))
                        split(WQKV, 2 * l + 2)
                    if l != 1 and batches[0] == 0:
                        dve.wait_ge(m_gate[gate_par], 64 * (NM // 2 * l + gr + 1))
                    for s in batches:
                        n = (n_unit(l) + EXPERTS[l] * m + e) * MT + s
                        ps = PS[6 + s % 2][:, 0:C]
                        dve.wait_ge(f2_done, n + 1)
                        a = acc[:, s * C:(s + 1) * C]
                        if l != 1:
                            V.tensor_tensor(a, ps, mgate[:, gate_par, s * C:(s + 1) * C], ALU.mult).then_inc(acc_done, 1)
                        elif e == 0:
                            V.tensor_scalar(a, ps, cw[:, s * NE:s * NE + 1], None, ALU.mult).then_inc(acc_done, 1)
                        else:
                            V.scalar_tensor_tensor(a, ps, cw[:, s * NE + e:s * NE + e + 1], a, ALU.mult, ALU.add).then_inc(acc_done, 1)

                def mlp_out(m, par, gr):
                    last_n = (n_unit(l) + EXPERTS[l] * (m + 1)) * MT
                    n0 = n_batch(l, 1) + MT * m
                    if l == 1:
                        dve.wait_ge(m_gate[par], 64 * (NM // 2 * l + gr + 1))
                    dve.wait_ge(acc_done, last_n)
                    if l == 1:
                        for s in range(MT):
                            gated(acc[:, s * C:(s + 1) * C], mgate[:, par, s * C:(s + 1) * C])
                            added(n_gated(l, 1) + MT * m + s, n0 + s, MT * m + s)
                    else:
                        for s in range(MT):
                            V.tensor_tensor(xb(MT * m + s), xb(MT * m + s), acc[:, s * C:(s + 1) * C], ALU.add).then_inc(x_new, 1)
                        for s in range(MT):
                            dve.wait_ge(x_new, n0 + s + 1)
                            dve.wait_ge(s_const, 1)
                            V.bn_stats(st6[:, cut(MT * m + s, 1), :], xb(MT * m + s)).then_inc(res_done, 1)

                mlp_rows(0, 0)
                mlp_low(0, 0)
                mlp_rows(1, 1)

                def mlp_step(m, par, gr, more1, more2):
                    router(m)
                    for e in range(EXPERTS[l]):
                        expert_sums(m, e, range(MT), not more1 and e == EXPERTS[l] - 1 and l + 1 < LAYERS)
                        if e == 0 and more1:
                            mlp_low(m + 1, 1 - par)
                        if e == 0 and more2:
                            mlp_rows(m + 2, par)
                    mlp_out(m, par, gr)

                def dense_step(m, par, gr):
                    static = isinstance(m, int)
                    if not static or m + 2 < NM:
                        mlp_rows(m + 2, par)
                    out = not static or m > 0
                    if out:
                        gr_out = gr if par else gr - 1
                        expert_sums(m - 1, 0, range(2), False, 1 - par, gr_out)
                    if not static or m + 1 < NM:
                        mlp_low(m + 1, 1 - par)
                    if out:
                        expert_sums(m - 1, 0, range(2, MT), static and m == NM and l + 1 < LAYERS, 1 - par, gr_out)
                    if out:
                        mlp_out(m - 1, 1 - par, gr_out)

                if l == 1:
                    with dve.Fori(0, NM // 2 - 1) as i:
                        mlp_step(2 * i, 0, i, True, True)
                        mlp_step(2 * i + 1, 1, i, True, True)
                    mlp_step(NM - 2, 0, NM // 2 - 1, True, False)
                    mlp_step(NM - 1, 1, NM // 2 - 1, False, False)
                else:
                    dense_step(0, 0, 0)
                    dense_step(1, 1, 0)
                    with dve.Fori(1, NM // 2 - 1) as i:
                        dense_step(2 * i, 0, i)
                        dense_step(2 * i + 1, 1, i)
                    for m in range(NM - 2, NM + 1):
                        dense_step(m, m % 2, m // 2)
                dve.wait_ge(res_done, n_batch(l, 1) + NB)
            for c in range(0, 8, 2):
                dve.wait_ge(sk_ps, c + 1)
                V.tensor_copy(SV[:, c * 512:(c + 1) * 512], PS[c][0:NB, :]).then_inc(sk_ev0, 1)
            rev = [0]

            def stepped(ins):
                rev[0] += 1
                ins.then_inc(r_ev, 1)
                return rev[0]

            def flat(m):
                return m.rearrange("p n j -> p (n j)")

            def quarter(m, k):
                s, h = k // 2, k % 2
                return flat(m)[s * RD:(s + 1) * RD, h * 512:(h + 1) * 512]

            def bank(b0, k):
                return PS[b0 + k][(k // 2) * RD:(k // 2 + 1) * RD, :]

            RAW, A, A2, A3, A4, BE, BO, EE, EO = M[0], M[1], M[2], M[3], M[4], M[5], M[0], M[6], M[7]
            sgn = K[:, K_SGN:K_SGN + RD].rearrange("p (o j) -> p o j", o=1).broadcast_to([128, NHALF, RD])
            dve.wait_ge(sk_ld, 32)
            stepped(V.scalar_tensor_tensor(A, RAW, 2.0 ** -SQUARINGS, sgn, ALU.mult, ALU.mult))
            dve.wait_ge(r_ps, 1)
            for k in range(4):
                stepped(V.tensor_scalar(quarter(A2, k), bank(0, k), -1.0, None, ALU.mult))
            dve.wait_ge(r_ev, 5)
            stepped(V.tensor_scalar(flat(BE), flat(A2), 1 / 720, None, ALU.mult))
            dve.wait_ge(r_ps, 2)
            for k in range(4):
                stepped(V.tensor_scalar(quarter(A3, k), bank(4, k), -1.0, None, ALU.mult))
            dve.wait_ge(r_ps, 3)
            for k in range(4):
                stepped(V.tensor_copy(quarter(A4, k), bank(0, k)))
            dve.wait_ge(r_ev, 14)
            stepped(V.scalar_tensor_tensor(flat(BE), flat(A4), 1 / 40320, flat(BE), ALU.mult, ALU.add))
            stepped(V.tensor_scalar(flat(BO), flat(A), 1 / 120, None, ALU.mult))
            dve.wait_ge(r_ev, 16)
            stepped(V.scalar_tensor_tensor(flat(BO), flat(A3), 1 / 5040, flat(BO), ALU.mult, ALU.add))
            stepped(V.tensor_scalar(flat(EE), flat(A2), 0.5, None, ALU.mult))
            dve.wait_ge(r_ev, 18)
            stepped(V.scalar_tensor_tensor(flat(EE), flat(A4), 1 / 24, flat(EE), ALU.mult, ALU.add))
            stepped(V.scalar_tensor_tensor(flat(EO), flat(A3), 1 / 6, flat(A), ALU.mult, ALU.add))
            dve.wait_ge(r_ev, 20)
            dve.wait_ge(r_ps, 4)
            for k in range(4):
                stepped(V.tensor_tensor(quarter(EE, k), quarter(EE, k), bank(0, k), ALU.add))
            dve.wait_ge(r_ps, 5)
            for k in range(4):
                stepped(V.tensor_tensor(quarter(EO, k), quarter(EO, k), bank(4, k), ALU.add))
            dve.wait_ge(r_ev, 28)
            stepped(V.tensor_tensor(flat(FM[0]), flat(EE), flat(EO), ALU.add))
            stepped(V.tensor_tensor(flat(FM[1]), flat(EE), flat(EO), ALU.subtract))
            for q in range(SQUARINGS):
                old, new = (FM[0:2], FM[2:4]) if q % 2 == 0 else (FM[2:4], FM[0:2])
                dve.wait_ge(r_ev, 30 + 8 * q)
                for w in range(2 if q + 1 < SQUARINGS else 1):
                    dve.wait_ge(r_ps, 6 + 2 * q + w)
                    for k in range(4):
                        stepped(V.scalar_tensor_tensor(quarter(new[w], k), quarter(old[w], k), 2.0, bank(4 * w, k),
                                                       ALU.mult, ALU.add))
            dve.wait_ge(qr_done, 1)
            for k in range(2):
                last = V.tensor_copy(UD[:, :, k * RD:(k + 1) * RD], QU[:, :, :])
            last.then_inc(u_dup, 1)
            dve.wait_ge(u_ps, 1)
            V.tensor_copy(UT[:, :], PS[7][:, 0:C]).then_inc(u_ev, 1)

            def z_copy(q):
                s = q // (NM // 2)
                dve.wait_ge(z_ps, q + 1)
                wait(dve, yy_ps, q - 1)
                V.tensor_copy(zs[s * RD:(s + 1) * RD, (q % 2) * 512:(q % 2 + 1) * 512], PS[4][s * RD:(s + 1) * RD, :])\
                    .then_inc(z_ev, 1)

            def rotated(q):
                for h in range(2):
                    dve.wait_ge(o_ps, 2 * q + h + 1)
                    x2 = X[:, (MT * q + 2 * h) * C:(MT * q + 2 * h + 2) * C]
                    V.tensor_tensor(x2, x2, PS[6 + h][:, 0:2 * C], ALU.add).then_inc(o_ev, 1)

            for q in range(NM):
                z_copy(q)
                if q:
                    rotated(q - 1)
            rotated(NM - 1)

        @block.scalar
        def _(act):
            S = nc.scalar
            act.wait_ge(ld_cond, 80)
            S.activation(ctmp[:, 2, :], ctmp[:, 0, :], ACT.Exp, scale=-1.0).then_inc(s_e, 1)
            S.activation(ctmp[0:C - C0, 3, :], ctmp[0:C - C0, 1, :], ACT.Exp, scale=-1.0).then_inc(s_e, 1)
            act.wait_ge(s_const, 1)

            def root(l, mlp):
                act.wait_ge(s_var, 4 * (2 * l + mlp + 1))
                S.activation(rtmp[:, 0, :], var[:, :], ACT.Sqrt, bias=epst[:, l // 2:l // 2 + 1]).then_inc(s_std, 1)

            for l in range(LAYERS):
                root(l, 0)

                def h_modulate(P):
                    act.wait_ge(xt_done, n_h(l, 0) + P + 1)
                    wait(act, h_ready, n_h(l, 0) + P)
                    for s in range(2):
                        b = 2 * P + s
                        S.activation(hf[:, s * 128:(s + 1) * 128], PS[5][:, s * 128:(s + 1) * 128], ACT.Identity,
                                     scale=col0[:, l, 1, cut(b, 1)], bias=col0[:, l, 0, cut(b, 1)])
                        last = S.activation(hs[:, s * 128:(s + 1) * 128], PS[5][0:S3, 256 + s * 128:256 + (s + 1) * 128],
                                            ACT.Identity, scale=col1[:, l, 1, cut(b, 1)], bias=col1[:, l, 0, cut(b, 1)])
                    last.then_inc(hf_ready, 1)

                def h_high(P, par):
                    act.wait_ge(hf_ready, n_h(l, 0) + P + 1)
                    wait(act, v_ps, NB // 2 * l + P - 1)
                    S.activation(hhi[:, par, 0:256], hf[:, 0:256], ACT.Copy)
                    S.activation(hshi[:, 0:256], hs[:, 0:256], ACT.Copy).then_inc(hhi_ready, 1)

                def qk_high(n):
                    act.wait_ge(qk_ps, n + 1)
                    wait(act, qk_lo, n)
                    S.activation(qkhi[:, :], PS[4][:, :], ACT.Copy).then_inc(qk_hi, 1)

                def k_place(pn, par, j):
                    act.wait_ge(qk_lo, 4 * pn + j + 1)
                    for r in (0, 1):
                        rows = slice(HP * r, HP * (r + 1))
                        last = S.activation(KBD[rows, par, 2 * j:2 * j + 2, r, :],
                                            kst[rows, :].rearrange("p (g n) -> p g n", g=2), ACT.Copy)
                    last.then_inc(kbd_a, 1)

                def exps(b, u, g):
                    n = 4 * (NB * l + b) + g
                    act.wait_ge(s2_done, n + 1)
                    wait(act, pv_done, NB * l + b - 1)
                    S.activation(PT[:, u % 2, g, :], PS[2 + g % 2][:, :], ACT.Exp, scale=float(HD) ** -0.5).then_inc(exp_done, 1)

                def out_copy(b, u):
                    n = NB * l + b
                    act.wait_ge(pv_done, n + 1)
                    wait(act, otr_done, n - 1)
                    S.activation(OTs[:, u % 2, :], PS[6][:, :], ACT.Copy).then_inc(ot_ev, 1)

                def oT_copy(b, u):
                    n = NB * l + b
                    act.wait_ge(ot2_done, n + 1)
                    wait(act, y_done, n - 1)
                    S.activation(oT[:, u % 2, 0:128], PS[7][:, 0:128], ACT.Copy)
                    S.activation(oT[0:C1, u % 2, 128:256], PS[7][0:C1, 128:256], ACT.Copy).then_inc(oT_ev, 1)

                def step(t, u, i=None):
                    static = i is None
                    P, par, odd = (t // 2 if static else 2 * i + u // 2), u // 2, u % 2
                    pair_n = NB // 2 * l + P + 1
                    base = 4 * pair_n
                    live = not static or t < NB
                    nxt = not static or P + 1 < NB // 2
                    before = not static or 1 <= t <= NB
                    tail = not static or t >= 2
                    if tail:
                        out_copy(t - 2, u)
                    if before:
                        exps(t - 1, u + 1, 0)
                    if before:
                        exps(t - 1, u + 1, 1)
                    if live and odd and (not static or P + 2 < NB // 2):
                        h_modulate(P + 2)
                    if live and odd and nxt:
                        qk_high(base + 2)
                    if before:
                        exps(t - 1, u + 1, 2)
                    if before:
                        exps(t - 1, u + 1, 3)
                    if tail:
                        oT_copy(t - 2, u)
                    if live and nxt:
                        qk_high(base + (3 if odd else 0))
                    if live and odd and nxt:
                        k_place(pair_n, 1 - par, 1)
                    if live and odd and (not static or P + 2 < NB // 2):
                        h_high(P + 2, par)
                    if live and not odd and nxt:
                        k_place(pair_n, 1 - par, 0)
                        qk_high(base + 1)

                h_modulate(0)
                h_high(0, 0)
                for j in range(4):
                    qk_high(4 * (NB // 2) * l + j)
                    if j < 2:
                        k_place(NB // 2 * l, 0, j)
                h_modulate(1)
                h_high(1, 1)
                for t in range(4):
                    step(t, t)
                with act.Fori(1, NB // 4 - 1) as i:
                    for u in range(4):
                        step(4 * i + u, u, i)
                for t in range(NB - 4, NB + 2):
                    step(t, t % 4)

                root(l, 1)
                gelu = ACT.Gelu if l == 2 else ACT.Gelu_apprx_tanh

                def mlp_high(m, par):
                    act.wait_ge(xt_done, n_h(l, 1) + m + 1)
                    wait(act, h_ready, n_h(l, 1) + m)
                    for s in range(MT):
                        b, at = MT * m + s, slice(s * 128, (s + 1) * 128)
                        S.activation(hf[:, at], PS[5][:, at], ACT.Identity,
                                     scale=col0[:, l, 3, cut(b, 1)], bias=col0[:, l, 2, cut(b, 1)])
                        last = S.activation(hs[:, at], PS[4][0:S3, at], ACT.Identity,
                                            scale=col1[:, l, 3, cut(b, 1)], bias=col1[:, l, 2, cut(b, 1)])
                    last.then_inc(hf_ready, 1)
                    act.wait_ge(hf_ready, n_h(l, 1) + m + 1)
                    wait(act, f1_done, n_f1(l) + FTOT[l] * (m - 1))
                    S.activation(hhi[:, par, :], hf[:, :], ACT.Copy)
                    S.activation(hshi[:, :], hs[:, :], ACT.Copy).then_inc(hhi_ready, 1)

                def gelus(m, par, e, part=None):
                    j0 = sum(FTILES[l][:e])
                    for j in part or range(j0, j0 + FTILES[l][e]):
                        n = n_f1(l) + FTOT[l] * m + j
                        act.wait_ge(f1_done, n + 1)
                        wait(act, f2_done, (n_unit(l) + (4 * m if l == 1 else m - 1)) * MT)
                        rows = 64 if l != 1 and j == 4 else 128
                        slot = j if l == 1 else 5 * par + j
                        S.activation(hm[0:rows, slot, :], PS[(par * FTOT[l] + j) % 2][0:rows, :], gelu).then_inc(gelu_done, 1)

                def mlp_step(m, par, more):
                    gelus(m, par, 0)
                    gelus(m, par, 1)
                    act.wait_ge(g_steps, 12 * m + 10)
                    S.activation(rt[:, 236:240], rt[:, 232:236], ACT.Tanh).then_inc(g_th, 1)
                    if more:
                        mlp_high(m + 1, 1 - par)
                    for e in range(2, EXPERTS[l]):
                        gelus(m, par, e)

                def dense_step(m, par):
                    gelus(m, par, 0, range(2))
                    if not isinstance(m, int) or m + 1 < NM:
                        mlp_high(m + 1, 1 - par)
                    gelus(m, par, 0, range(2, FT))

                mlp_high(0, 0)
                if l == 1:
                    with act.Fori(0, NM // 2 - 1) as i:
                        mlp_step(2 * i, 0, True)
                        mlp_step(2 * i + 1, 1, True)
                    mlp_step(NM - 2, 0, True)
                    mlp_step(NM - 1, 1, False)
                else:
                    dense_step(0, 0)
                    dense_step(1, 1)
                    with act.Fori(1, NM // 2 - 1) as i:
                        dense_step(2 * i, 0)
                        dense_step(2 * i + 1, 1)
                    dense_step(NM - 2, 0)
                    dense_step(NM - 1, 1)
            for c in range(1, 8, 2):
                act.wait_ge(sk_ps, c + 1)
                S.activation(SV[:, c * 512:(c + 1) * 512], PS[c][0:NB, :], ACT.Copy).then_inc(sk_ev1, 1)

            def x_copy(q):
                act.wait_ge(t_ps, q + 1)
                wait(act, z_ps, q - 1)
                at = (q % 2) * 512
                S.activation(xT0[:, at:at + 512], PS[2 * (q % 2)][:, :], ACT.Copy)
                S.activation(xT1[:, at:at + 512], PS[2 * (q % 2) + 1][0:C - C0, :], ACT.Copy).then_inc(t_ev, 1)

            act.wait_ge(u_ps, 1)
            x_copy(0)
            for q in range(NM):
                if q + 1 < NM:
                    x_copy(q + 1)
                s = q // (NM // 2)
                act.wait_ge(yy_ps, q + 1)
                wait(act, o_ps, 2 * (q - 1))
                S.activation(ys[s * RD:(s + 1) * RD, (q % 2) * 512:(q % 2 + 1) * 512], PS[5][s * RD:(s + 1) * RD, :],
                             ACT.Copy).then_inc(yy_ev, 1)

        @block.tensor
        def _(pe):
            mm = nc.tensor.matmul
            pe.wait_ge(s_silu, 4)
            pe.wait_ge(ld_gw, 32)
            for n in range(2):
                lo, hi = n * GC // 2, (n + 1) * GC // 2
                mm(PS[n][0:NB, 0:GC // 2], sc0[:, :], BIG[:, lo:hi], start=True, stop=False)
                mm(PS[n][0:NB, 0:GC // 2], sc1[:, :], BIG[0:C1, GC + lo:GC + hi], start=False, stop=True).then_inc(s_gps, 1)
            pe.wait_ge(ld_ada, 32)
            A0, A1 = 2 * GC, 2 * GC + LAYERS * 4 * XW
            for l in range(LAYERS):
                if l == 2:
                    pe.wait_ge(s_cev, 1)
                for kind in range(4):
                    at = (4 * l + kind) * XW
                    for ps, off, rows in ((PS[2 + 2 * (l % 2)], 0, C0), (PS[3 + 2 * (l % 2)], C0, S3)):
                        o = ps[0:rows, kind * NB:(kind + 1) * NB]
                        mm(o, BIG[:, A0 + at + off:A0 + at + off + rows], sc0[:, :], start=True, stop=False)
                        last = mm(o, BIG[0:C1, A1 + at + off:A1 + at + off + rows], sc1[:, :], start=False, stop=True)
                last.then_inc(s_cps, 1)

            def split_product(o, w, h0, par, n0, n, weights_moving=False):
                pairs = ((Whi[:, w], hhi[:, par, n0:n0 + n]), (Wlo[:, w], hhi[:, par, n0:n0 + n]),
                         (Whi[:, w], hlo[:, par, n0:n0 + n]), (W3[:, w], h3[:, par, n0:n0 + n]))
                for k, (a, b) in enumerate(pairs):
                    if weights_moving:
                        a, b = b, a
                    last = mm(o, a, b, start=(k == 0), stop=(k == 3))
                return last

            for l in range(LAYERS):
                pe.wait_ge(s_split, SPLITS * (2 * l + 1))
                pe.wait_ge(ld_wp, 32 * (l + 1))
                if l == 0:
                    pe.wait_ge(s_cev, LAYERS)
                else:
                    pe.wait_ge(res_done, n_batch(l, 0))

                def turn(P, par):
                    pe.wait_ge(xh_ready, n_batch(l, 0) + 2 * P + 2)
                    for s in range(2):
                        slot = 2 * par + s
                        nc.tensor.transpose(PS[5][:, s * 128:(s + 1) * 128], xh[:, slot, 0:C0], ident)
                        last = nc.tensor.transpose(PS[5][0:S3, 256 + s * 128:256 + (s + 1) * 128], xh[:, slot, C0:XW], ident)
                    last.then_inc(xt_done, 1)

                def qk_product(P, par, j):
                    n = 4 * (NB // 2 * l + P) + j
                    if j == 0:
                        pe.wait_ge(h_ready, n_h(l, 0) + P + 1)
                    wait(pe, qk_lo, n)
                    for gg in range(2):
                        g = 2 * (j % 2) + gg
                        w0 = (1 - j // 2) * G * 128 + g * 128
                        last = split_product(PS[4][:, gg * 256:(gg + 1) * 256], slice(w0, w0 + 128), None, par, 0, 256)
                    last.then_inc(qk_ps, 1)

                def v_product(P, par):
                    for s in range(2):
                        last = split_product(PS[5][:, s * C:(s + 1) * C], slice(2 * G * 128, WQKV), None, par, s * 128, 128,
                                             weights_moving=True)
                    last.then_inc(v_ps, 1)

                def s1(b, u, g):
                    n = 4 * (NB * l + b) + g
                    wait(pe, max_done, n - 1)
                    q0 = (u % 2) * 128
                    mm(PS[g % 2][:, :], Q[:, u // 2, g, q0:q0 + 128], KBD[:, u // 2, g, :, q0:q0 + 128],
                       start=True, stop=True).then_inc(s1_done, 1)

                def s2(b, u, g):
                    n = 4 * (NB * l + b) + g
                    wait(pe, exp_done, n - 1)
                    if g == 0:
                        pe.wait_ge(mrow, NB * l + b + 1)
                    q0 = (u % 2) * 128
                    for r in range(HG):
                        last = mm(PS[2 + g % 2][:, r * 128:(r + 1) * 128], KBD[:, u // 2, g, r, q0:q0 + 128],
                                  Q[:, u // 2, g, q0:q0 + 128], start=True, stop=True)
                    last.then_inc(s2_done, 1)

                def pv(b, u, g, vn):
                    n = NB * l + b
                    if g == 0:
                        wait(pe, ot_ev, n)
                        pe.wait_ge(v_ev, vn)
                    pe.wait_ge(exp_done, 4 * n + g + 1)
                    for r in range(HG):
                        last = mm(PS[6][HP * r:HP * (r + 1), g * 128:(g + 1) * 128], VA[:, u, G * g + r, :],
                                  PT[:, u % 2, g, r * 128:(r + 1) * 128], start=True, stop=True)
                    if g == G - 1:
                        last.then_inc(pv_done, 1)

                def max_turn(b, u):
                    pe.wait_ge(max_done, 4 * (NB * l + b + 1))
                    for g in range(G):
                        last = nc.tensor.transpose(PS[5][:, g * 128:(g + 1) * 128], nmax[:, g, :], ident)
                    last.then_inc(mt_done, 1)

                def out_back(b, u):
                    n = NB * l + b
                    pe.wait_ge(ot_ev, n + 1)
                    wait(pe, y_read, n_gated(l, 0) + b)
                    for g in range(G):
                        last = nc.tensor.transpose(PS[7][:, g * 128:(g + 1) * 128], OTs[:, u % 2, g * 128:(g + 1) * 128], ident)
                    last.then_inc(otr_done, 1)

                def out_turn(b, u):
                    pe.wait_ge(norm_done, NB * l + b + 1)
                    nc.tensor.transpose(PS[7][:, 0:128], oq[:, u % 2, 0:C0], ident)
                    nc.tensor.transpose(PS[7][0:C1, 128:256], oq[:, u % 2, C0:C + 1], ident).then_inc(ot2_done, 1)

                def project(b, u):
                    pe.wait_ge(oT_ev, NB * l + b + 1)
                    mm(PS[7][:, 0:C], oT[:, u % 2, 0:128], wp0[:, l % 2, :], start=True, stop=False)
                    mm(PS[7][:, 0:C], oT[0:C1, u % 2, 128:256], wp1[:, l % 2, :], start=False, stop=True).then_inc(y_done, 1)

                def step(t, u, i=None):
                    static = i is None
                    P, par, odd = (t // 2 if static else 2 * i + u // 2), u // 2, u % 2
                    live = not static or t < NB
                    nxt = not static or P + 1 < NB // 2
                    nxt2 = not static or P + 2 < NB // 2
                    before = not static or 1 <= t <= NB
                    tail = not static or t >= 2
                    u1, u2 = (u + 3) % 4, (u + 2) % 4
                    if live and not odd:
                        pe.wait_ge(kbd_a, 2 * (NB // 2 * l + P + 1))
                        pe.wait_ge(kbd_v, 2 * (NB // 2 * l + P + 1))
                        pe.wait_ge(qk_lo, 4 * (NB // 2 * l + P + 1))
                    if live:
                        s1(t, u, 0)
                    if before:
                        s2(t - 1, u1, 0)
                    if live and odd and nxt2:
                        turn(P + 2, par)
                    if live:
                        s1(t, u, 1)
                    if before:
                        s2(t - 1, u1, 1)
                    if tail:
                        out_back(t - 2, u2)
                    if live and not odd and not (static and t == 0):
                        v_product(P, par)
                    if live:
                        s1(t, u, 2)
                    if live and odd and nxt:
                        qk_product(P + 1, 1 - par, 2)
                    if before:
                        s2(t - 1, u1, 2)
                    if live:
                        s1(t, u, 3)
                    if before:
                        s2(t - 1, u1, 3)
                    if tail:
                        out_turn(t - 2, u2)
                    if live and nxt:
                        qk_product(P + 1, 1 - par, 3 if odd else 0)
                    vn = None if not before else (NB // 2 * l + ((t - 1) // 2 if static else (2 * i + u // 2 - (0 if odd else 1))) + 1)
                    if before:
                        pv(t - 1, u1, 0, vn)
                        pv(t - 1, u1, 1, vn)
                    if live:
                        pe.wait_ge(v_ev, NB // 2 * l + P + 1)
                        if odd and nxt2:
                            pe.wait_ge(hf_ready, n_h(l, 0) + P + 3)
                        max_turn(t, u)
                    if tail:
                        project(t - 2, u2)
                    if before:
                        pv(t - 1, u1, 2, vn)
                        pv(t - 1, u1, 3, vn)
                    if live and not odd and nxt:
                        qk_product(P + 1, 1 - par, 1)

                turn(0, 0)
                for j in range(4):
                    qk_product(0, 0, j)
                v_product(0, 0)
                pe.wait_ge(v_ev, NB // 2 * l + 1)
                turn(1, 1)
                pe.wait_ge(va_set, 3 * (l + 1))
                pe.wait_ge(hf_ready, n_h(l, 0) + 2)
                for t in range(4):
                    step(t, t)
                with pe.Fori(1, NB // 4 - 1) as i:
                    for u in range(4):
                        step(4 * i + u, u, i)
                for t in range(NB - 4, NB + 2):
                    step(t, t % 4)

                pe.wait_ge(s_split, SPLITS * (2 * l + 2))
                pe.wait_ge(ld_w2, (16, 48, 64)[l])
                pe.wait_ge(res_done, n_batch(l, 1))
                if l != 1:
                    pe.wait_ge(hm_ones, 1 if l == 0 else 2)

                def turn_rows(m, par):
                    pe.wait_ge(xh_ready, n_batch(l, 1) + MT * (m + 1))
                    wait(pe, hf_ready, n_h(l, 1) + m)
                    for s in range(MT):
                        slot = MT * par + s
                        nc.tensor.transpose(PS[5][:, s * 128:(s + 1) * 128], xh[:, slot, 0:C0], ident)
                        last = nc.tensor.transpose(PS[4][0:S3, s * 128:(s + 1) * 128], xh[:, slot, C0:XW], ident)
                    last.then_inc(xt_done, 1)

                def first(m, par, e, part=None):
                    j0 = sum(FTILES[l][:e])
                    for j in range(j0, j0 + FTILES[l][e]) if part is None else (j0 + part,):
                        n = n_f1(l) + FTOT[l] * m + j
                        wait(pe, gelu_done, n - 1)
                        rows = 64 if l != 1 and j == 4 else 128
                        w0 = 128 * j
                        split_product(PS[(par * FTOT[l] + j) % 2][0:rows, :], slice(w0, w0 + rows), None, par, 0, 512)\
                            .then_inc(f1_done, 1)

                def router(m, par):
                    for s in range(MT):
                        last = split_product(PS[2][:, s * NE:(s + 1) * NE], slice(NE * FF, WM[1]), None, par,
                                             s * 128, 128, weights_moving=True)
                    last.then_inc(g_ps, 1)

                def second(m, par, e, part=None):
                    t0 = (9 * e) // 2
                    pe.wait_ge(gelu_done, n_f1(l) + FTOT[l] * m + min(t0 + FT, FTOT[l]))
                    for s in range(MT) if part is None else (part,):
                        n = (n_unit(l) + EXPERTS[l] * m + e) * MT + s
                        wait(pe, acc_done, n - 1)
                        o = PS[6 + s % 2][:, 0:C]
                        for k in range(FT):
                            slot = t0 + k if l == 1 else 5 * par + k
                            rows = 65 if l != 1 and k == FT - 1 else 128
                            last = mm(o, hm[0:rows, slot, s * 128:(s + 1) * 128], w2[0:rows, FT * e + k, :],
                                      start=(k == 0), stop=(l != 1 and k == FT - 1))
                        if l == 1:
                            last = mm(o, ones[0:1, :], b2[0:1, e, :], start=False, stop=True)
                        last.then_inc(f2_done, 1)

                def mlp_step(m, par, more):
                    pe.wait_ge(h_ready, n_h(l, 1) + m + 1)
                    first(m, par, 0)
                    router(m, par)
                    if more:
                        turn_rows(m + 1, 1 - par)
                    for e in range(1, EXPERTS[l]):
                        first(m, par, e)
                        second(m, par, e - 1)
                    second(m, par, EXPERTS[l] - 1)

                def dense_step(m, par):
                    static = isinstance(m, int)
                    if not static or m + 1 < NM:
                        turn_rows(m + 1, 1 - par)
                    if not static or m < NM:
                        pe.wait_ge(h_ready, n_h(l, 1) + m + 1)
                    for k in range(FT):
                        if not static or m < NM:
                            first(m, par, 0, k)
                        if k < MT and (not static or m > 0):
                            second(m - 1, 1 - par, 0, k)

                turn_rows(0, 0)
                if l == 1:
                    with pe.Fori(0, NM // 2 - 1) as i:
                        mlp_step(2 * i, 0, True)
                        mlp_step(2 * i + 1, 1, True)
                    mlp_step(NM - 2, 0, True)
                    mlp_step(NM - 1, 1, False)
                else:
                    dense_step(0, 0)
                    dense_step(1, 1)
                    with pe.Fori(1, NM // 2 - 1) as i:
                        dense_step(2 * i, 0)
                        dense_step(2 * i + 1, 1)
                    for m in range(NM - 2, NM + 1):
                        dense_step(m, m % 2)
            pe.wait_ge(res_done, n_batch(LAYERS, 0))
            pe.wait_ge(ld_skew, 32)
            for c in range(8):
                mm(PS[c][0:NB, :], sc0[:, :], SW0[:, c * 512:(c + 1) * 512], start=True, stop=False)
                mm(PS[c][0:NB, :], sc1[:, :], SW1[:, c * 512:(c + 1) * 512], start=False, stop=True).then_inc(sk_ps, 1)

            def matrices(b0, a, b):
                for s in range(2):
                    rows = slice(s * RD, (s + 1) * RD)
                    for n in range(NHALF):
                        at = (n % 8) * RD
                        last = mm(PS[b0 + 2 * s + n // 8][rows, at:at + RD], a[rows, n, :], b[rows, n, :], start=True, stop=True)
                last.then_inc(r_ps, 1)

            A, A2, A3, A4, BE, BO = M[1], M[2], M[3], M[4], M[5], M[0]
            pe.wait_ge(sk_ev0, 4)
            pe.wait_ge(sk_ev1, 4)
            pe.wait_ge(r_ev, 1)
            matrices(0, A, A)
            pe.wait_ge(r_ev, 5)
            matrices(4, A, A2)
            matrices(0, A2, A2)
            pe.wait_ge(r_ev, 15)
            matrices(0, A4, BE)
            pe.wait_ge(r_ev, 17)
            matrices(4, A4, BO)
            pe.wait_ge(r_ev, 30)
            for q in range(SQUARINGS):
                F, F_T = (FM[0:2] if q % 2 == 0 else FM[2:4])
                if q:
                    pe.wait_ge(r_ev, 30 + 8 * q)
                matrices(0, F_T, F)
                if q + 1 < SQUARINGS:
                    matrices(4, F, F_T)
            F = FM[0] if SQUARINGS % 2 == 0 else FM[2]
            pe.wait_ge(u_dup, 1)
            pe.wait_ge(r_ev, 30 + 8 * SQUARINGS - 4)
            nc.tensor.transpose(PS[7][:, 0:C0], UD[:, 0, :], ident)
            nc.tensor.transpose(PS[7][:, C0:C], UD[0:C - C0, 1, :], ident[0:C - C0, 0:C - C0]).then_inc(u_ps, 1)

            def x_turn(q):
                wait(pe, t_ev, q - 1)
                for s in range(MT):
                    b = MT * q + s
                    nc.tensor.transpose(PS[2 * (q % 2)][:, s * 128:(s + 1) * 128], X[:, b * C:b * C + C0], ident)
                    last = nc.tensor.transpose(PS[2 * (q % 2) + 1][0:C - C0, s * 128:(s + 1) * 128],
                                               X[:, b * C + C0:(b + 1) * C], ident)
                last.then_inc(t_ps, 1)

            def z_product(q):
                rows, at = slice((q // 4) * RD, (q // 4 + 1) * RD), (q % 2) * 512
                pe.wait_ge(t_ev, q + 1)
                wait(pe, z_ev, q)
                mm(PS[4][rows, :], QU[:, 0, :], xT0[:, at:at + 512], start=True, stop=False)
                mm(PS[4][rows, :], QU[0:C - C0, 1, :], xT1[:, at:at + 512], start=False, stop=True).then_inc(z_ps, 1)

            def zr_product(q):
                rows, at = slice((q // 4) * RD, (q // 4 + 1) * RD), (q % 2) * 512
                pe.wait_ge(z_ev, q + 1)
                wait(pe, yy_ev, q)
                for s in range(MT):
                    last = mm(PS[5][rows, s * 128:(s + 1) * 128], F[rows, (MT * q + s) % NHALF, :],
                              zs[rows, at + s * 128:at + (s + 1) * 128], start=True, stop=True)
                last.then_inc(yy_ps, 1)

            def back(q):
                rows, at = slice((q // 4) * RD, (q // 4 + 1) * RD), (q % 2) * 512
                pe.wait_ge(yy_ev, q + 1)
                for h in range(2):
                    wait(pe, o_ev, 2 * q + h - 1)
                    for s in (2 * h, 2 * h + 1):
                        last = mm(PS[6 + h][:, (s % 2) * C:(s % 2 + 1) * C], ys[rows, at + s * 128:at + (s + 1) * 128],
                                  UT[rows, :], start=True, stop=True)
                    last.then_inc(o_ps, 1)

            pe.wait_ge(u_ev, 1)
            x_turn(0)
            for q in range(NM):
                z_product(q)
                if q + 1 < NM:
                    x_turn(q + 1)
                zr_product(q)
                if q:
                    back(q - 1)
            back(NM - 1)

        @block.gpsimd
        def _(pool):
            R = nc.gpsimd
            pool.dma_start(QA[:, 0, :], d["P"][0:C0, :]).then_inc(q_ld, 16)
            R.memset(QA[:, 1, :], 0.0)
            R.memset(QU[:, 1, :], 0.0)
            R.memset(qk_[:, :], 0.0)
            R.memset(qc[:, 0:1], 0.5)
            R.memset(qc[:, 1:2], -1.0).then_inc(q_step, 1)
            pool.wait_ge(q_step, 1)
            pool.dma_start(QA[0:C - C0, 1, :], d["P"][C0:C, :]).then_inc(q_ld, 16)
            pool.wait_ge(ld_cond, 80)
            R.tensor_copy(QU[:, 0, :], K[:, K_EYE:K_EYE + RD]).then_inc(q_step, 1)
            pool.wait_ge(q_step, 2)
            pool.sem_clear(q_step)
            pool.wait_ge(q_ld, 32)
            iota = K[:, K_IOTA:K_IOTA + 1]

            def rows(a):
                return a.rearrange("p (o j) -> p o j", o=1).broadcast_to([128, 2, RD])

            def link(ins, value):
                ins.then_inc(q_step, 1)
                pool.wait_ge(q_step, value)

            with pool.Fori(0, RD) as k:
                ak, vk = QA[:, :, bass.ds(k, 1)], QV[:, :, bass.ds(k, 1)]
                R.tensor_scalar(qs[:, 0:1], iota, qk_[:, 0:1], None, ALU.is_ge)
                link(R.tensor_scalar(qs[:, 1:2], iota, qk_[:, 0:1], None, ALU.is_equal), 1)
                R.tensor_tensor(QV[:, 0, bass.ds(k, 1)], QA[:, 0, bass.ds(k, 1)], qs[:, 0:1], ALU.mult)
                R.tensor_copy(QV[:, 1, bass.ds(k, 1)], QA[:, 1, bass.ds(k, 1)])
                link(R.tensor_scalar(qprod[:, RD:2 * RD], QA[:, 0, :], qs[:, 1:2], None, ALU.mult), 2)
                link(R.tensor_tensor(qtmp[:, :, :], QA[:, :, :], vk.broadcast_to([128, 2, RD]), ALU.mult), 3)
                link(R.tensor_tensor(qprod[:, 0:RD], qtmp[:, 0, :], qtmp[:, 1, :], ALU.add), 4)
                link(R.partition_all_reduce(qsum[:, :], qprod[:, :], 128, RADD), 5)
                sq, al = qsum[:, bass.ds(k, 1)], qsum[:, bass.ds(k + RD, 1)]
                R.tensor_tensor(qs[:, 2:3], sq, qc[:, 0:1], ALU.pow)
                link(R.tensor_copy(qs[:, 3:4], al), 6)
                link(R.tensor_scalar(qs[:, 3:4], qs[:, 3:4], 0.0, 2.0, ALU.is_ge, ALU.mult), 7)
                link(R.tensor_scalar(qs[:, 4:5], qs[:, 3:4], -1.0, qs[:, 2:3], ALU.add, ALU.mult), 8)
                R.tensor_scalar(qs[:, 7:8], qs[:, 1:2], qs[:, 4:5], None, ALU.mult)
                R.tensor_scalar(qw[:, :], qsum[:, RD:2 * RD], qs[:, 4:5], None, ALU.mult)
                link(R.tensor_tensor(qs[:, 5:6], qs[:, 4:5], al, ALU.mult), 9)
                R.tensor_tensor(QV[:, 0, bass.ds(k, 1)], QV[:, 0, bass.ds(k, 1)], qs[:, 7:8], ALU.add)
                R.tensor_tensor(qw[:, :], qw[:, :], qsum[:, 0:RD], ALU.add)
                link(R.tensor_tensor(qs[:, 5:6], qs[:, 5:6], sq, ALU.add), 10)
                link(R.tensor_scalar(qs[:, 6:7], qs[:, 5:6], 1e-37, None, ALU.max), 11)
                link(R.tensor_tensor(qtau[:, bass.ds(k, 1)], qs[:, 6:7], qc[:, 1:2], ALU.pow), 12)
                link(R.tensor_tensor(qw[:, :], qw[:, :], qtau[:, bass.ds(k, 1)].broadcast_to([128, RD]), ALU.mult), 13)
                link(R.tensor_tensor(qtmp[:, :, :], vk.broadcast_to([128, 2, RD]), rows(qw[:, :]), ALU.mult), 14)
                R.tensor_scalar(qk_[:, :], qk_[:, :], 1.0, None, ALU.add)
                link(R.tensor_tensor(QA[:, :, :], QA[:, :, :], qtmp[:, :, :], ALU.subtract), FWD)
                pool.sem_clear(q_step)
            with pool.Fori(0, RD) as k:
                j = RD - 1 - k
                vj = QV[:, :, bass.ds(j, 1)].broadcast_to([128, 2, RD])
                link(R.tensor_tensor(qtmp[:, :, :], QU[:, :, :], vj, ALU.mult), 1)
                link(R.tensor_tensor(qprod[:, 0:RD], qtmp[:, 0, :], qtmp[:, 1, :], ALU.add), 2)
                link(R.partition_all_reduce(qsum[:, 0:RD], qprod[:, 0:RD], 128, RADD), 3)
                link(R.tensor_tensor(qw[:, :], qsum[:, 0:RD], qtau[:, bass.ds(j, 1)].broadcast_to([128, RD]), ALU.mult), 4)
                link(R.tensor_tensor(qtmp[:, :, :], vj, rows(qw[:, :]), ALU.mult), 5)
                link(R.tensor_tensor(QU[:, :, :], QU[:, :, :], qtmp[:, :, :], ALU.subtract), BWD)
                pool.sem_clear(q_step)
            R.memset(qk_[:, :], 0.0).then_inc(qr_done, 1)


def _pad_heads(w, b, row_one):
    wb = np.concatenate([w, b[None]], 0).reshape(C + 1, G, HG, HD)
    o = np.zeros((C + 1, G, HG, HP), np.float32)
    for k in range(3):
        o[:, :, :, k * HD:(k + 1) * HD] = wb
    if row_one:
        o[C, :, :, 3 * HD] = 1.0
    return o.reshape(C + 1, G * 128)


def _constants():
    k = np.zeros((128, K_N), np.float32)
    k[:, K_ID:K_ID + 128] = np.eye(128)
    p = np.arange(128)
    k[:, K_MQ] = -((p % HP >= 2 * HD) & (p % HP < 3 * HD)).astype(np.float32)
    k[:, K_MK] = -((p % HP >= HD) & (p % HP < 2 * HD)).astype(np.float32)
    k[:, K_MH] = -((p >= 2 * C1) & (p < S3)).astype(np.float32)
    k[:, K_MW] = -((p >= C1) & (p < 2 * C1)).astype(np.float32)
    k[:, K_IOTA] = p
    k[:RD, K_EYE:K_EYE + RD] = np.eye(RD)
    j = np.arange(RD)
    k[:, K_SGN:K_SGN + RD] = np.sign(j[None] - (p % RD)[:, None])
    k[:, K_LOW:] = (j[None, :NE] < j[:NE, None]).reshape(-1)
    return k


def _layout(a):
    z = np.zeros
    r = {"x": a["x"], "cond_t": a["cond_1152"].T, "consts": _constants()}
    ada = [(a["L0_cond_W_ada"], a["L0_cond_b_ada"]), (a["L1_cond_w_adaln"], a["L1_cond_b_adaln"]),
           (a["L2_cond_ada_w"], a["L2_cond_ada_b"])]
    gates, cols = [], []
    for w, b in ada:
        wb = np.concatenate([w, b[None]], 0).reshape(C + 1, 6, C)
        gates += [wb[:, 2], wb[:, 5]]
        for kind in (0, 1, 3, 4):
            t = z((C + 1, 3, C1), np.float32)
            t[:, :, :C - C0] = wb[:, kind, None, C0:]
            cols += [wb[:, kind, :C0], t.reshape(C + 1, S3)]
    r["ada_gate"] = np.concatenate(gates, 1)
    r["ada_col"] = np.concatenate(cols, 1)
    lc = z((XW, 4), np.float32)
    for n, name in enumerate(("ln1_w", "ln1_b", "ln2_w", "ln2_b")):
        v = a["L2_cond_" + name]
        t = np.full((3, C1), 1.0 - n % 2, np.float32)
        t[:, :C - C0] = v[C0:]
        lc[:, n] = np.concatenate([v[:C0], t.reshape(-1)])
    r["ln_col"] = lc
    zero = z((C,), np.float32)

    def split3(w, b):
        return [w[:, k * C:(k + 1) * C] for k in range(3)], [b[k * C:(k + 1) * C] for k in range(3)]

    qkv = [split3(a["L0_cond_W_qkv"], a["L0_cond_b_qkv"]), split3(a["L1_cond_w_qkv"], a["L1_cond_b_qkv"]),
           ([a["L2_cond_wq"], a["L2_cond_wk"], a["L2_cond_wv"]], [zero] * 3)]
    for l, (w, b) in enumerate(qkv):
        r[f"wqkv{l}"] = np.concatenate([_pad_heads(w[0], b[0], False), _pad_heads(w[1], b[1], True),
                                        np.concatenate([w[2], b[2][None]], 0)], 1)
    for l, (w, b) in enumerate(((a["L0_cond_W_proj"], a["L0_cond_b_proj"]), (a["L1_cond_w_proj"], a["L1_cond_b_proj"]),
                                (a["L2_cond_wo"], a["L2_cond_wo_b"]))):
        r[f"wp{l}"] = np.concatenate([w, b[None]], 0)
    for l, w1, b1, w2, b2 in ((0, "W_fc1", "b_fc1", "W_fc2", "b_fc2"), (2, "fc1_w", "fc1_b", "fc2_w", "fc2_b")):
        w1, b1, w2, b2 = (a[f"L{l}_cond_{n}"] for n in (w1, b1, w2, b2))
        r[f"wm{l}"] = np.concatenate([w1, b1[None]], 0)
        t = z((FT * 128, C), np.float32)
        t[:FF] = w2
        t[FF] = b2
        r[f"w2_{l}"] = t
    w1 = np.concatenate([a["L1_cond_w1"], a["L1_cond_b1"][:, None]], 1)
    wg = np.concatenate([a["L1_cond_w_gate"], z((1, NE), np.float32)], 0)
    r["wm1"] = np.concatenate([w1.transpose(1, 0, 2).reshape(C + 1, NE * FF), wg], 1)
    t = z((NE, FT * 128, C), np.float32)
    for e in range(NE):
        at = (e % 2) * 64
        t[e, at:at + FF] = a["L1_cond_w2"][e]
    r["w2_1"] = t.reshape(NE * FT * 128, C)
    r["b2_1"] = a["L1_cond_b2"][None]
    iu, ju = np.triu_indices(RD, k=1)
    wb = np.concatenate([a["L3_cond_W"].T, a["L3_cond_b"][None]], 0)
    t = z((C + 1, RD, RD), np.float32)
    t[:, iu, ju] = wb
    t[:, ju, iu] = wb
    r["skew_w"] = t.reshape(C + 1, RD * RD)
    r["P"] = a["L3_cond_P"]
    return {k: np.ascontiguousarray(v) for k, v in r.items()}


def kernel(**inputs):
    import concourse.bacc as _bacc
    from concourse.bass_utils import run_bass_kernel_spmd as _run

    nc = _bacc.Bacc("TRN2", target_bir_lowering=False, num_devices=1)
    arrays, d = {}, {}
    for name, a in _layout({k: np.asarray(v) for k, v in inputs.items()}).items():
        arrays[f"in_{name}"] = a
        d[name] = nc.dram_tensor(f"in_{name}", a.shape, mybir.dt.from_np(a.dtype), kind="ExternalInput").ap()
    out = nc.dram_tensor("out_0", (NB, T, C), F32, kind="ExternalOutput").ap()
    gates_dram = nc.dram_tensor("gates", (NB, GC), F32, kind="Internal").ap()
    skew_dram = nc.dram_tensor("skew", (NB, RD * RD), F32, kind="Internal").ap()
    program(nc, d, out, gates_dram, skew_dram)
    r = _run(nc, [arrays], core_ids=[0])
    return r.results[0]["out_0"]
```
